# Optimizing a Trainium2 kernel written in Bass

```python
import numpy as np
import jax
import jax.numpy as jnp

def _softmax(x, axis=-1):
    return jax.nn.softmax(x, axis=axis)

def _gelu(x):
    return jax.nn.gelu(x, approximate=True)

def _silu(x):
    return jax.nn.silu(x)

def _sigmoid(x):
    return jax.nn.sigmoid(x)

def _layernorm(x, axis=-1, eps=1e-05):
    m = jnp.mean(x, axis=axis, keepdims=True)
    v = jnp.var(x, axis=axis, keepdims=True)
    return (x - m) / jnp.sqrt(v + eps)

def _scatter_add(tgt, idx, src, axis=0):
    return tgt.at[idx].add(src)

def _segment_sum(src, seg, n):
    return jax.ops.segment_sum(src, seg, n)
kernel_name = 'mk_rec_standalone_d1_rec_r8_4e9ec5'

def setup_inputs(seed: int=0):
    np.random.seed(seed)
    _w = jnp.asarray

    def _rec_inputs():
        import jax
        import jax.numpy as jnp
        _rk = jax.random.key(seed)
        r_price = jax.random.uniform(jax.random.fold_in(_rk, 1), (2048, 1), jnp.float32, 0.0, 99.9292)
        r_user_id = jax.random.randint(jax.random.fold_in(_rk, 2), (2048, 1), 72, 99964, jnp.int32)
        r_item_id = jax.random.randint(jax.random.fold_in(_rk, 3), (2048, 1), 29, 49981, jnp.int32)
        r_age = jax.random.randint(jax.random.fold_in(_rk, 4), (2048, 1), 0, 10, jnp.int32)
        r_gender = jax.random.randint(jax.random.fold_in(_rk, 5), (2048, 1), 0, 3, jnp.int32)
        r_city = jax.random.randint(jax.random.fold_in(_rk, 6), (2048, 1), 0, 100, jnp.int32)
        r_category = jax.random.randint(jax.random.fold_in(_rk, 7), (2048, 1), 0, 50, jnp.int32)
        r_brand = jax.random.randint(jax.random.fold_in(_rk, 8), (2048, 1), 0, 1000, jnp.int32)
        r_hour = jax.random.randint(jax.random.fold_in(_rk, 9), (2048, 1), 0, 24, jnp.int32)
        r_device = jax.random.randint(jax.random.fold_in(_rk, 10), (2048, 1), 0, 5, jnp.int32)
        return (r_price, r_user_id, r_item_id, r_age, r_gender, r_city, r_category, r_brand, r_hour, r_device)
    r_price, r_user_id, r_item_id, r_age, r_gender, r_city, r_category, r_brand, r_hour, r_device = _rec_inputs()

    def _L0_rec_setup():
        import jax, jax.numpy as jnp
        import numpy as np
        B = 256
        VOCABS = [12500, 6250, 10, 3, 100, 50, 1000, 24, 5]
        E = 16
        EMB_DIMS = [E, E, E // 2, E // 4, E // 2, E // 2, E // 2, E // 4, E // 4]
        NUM_FEATURES = sum(VOCABS) + 1
        DEEP_IN = sum(EMB_DIMS) + 1
        HIDDEN = [256, 128, 64]
        key = jax.random.key(seed)
        ks = iter(jax.random.split(key, 40))
        inp = {}
        names = ['user_id', 'item_id', 'age', 'gender', 'city', 'category', 'brand', 'hour', 'device']
        for name, v in zip(names, VOCABS):
            inp[name] = jax.random.randint(next(ks), (B, 1), 0, v, dtype=jnp.int32).astype(jnp.int64)
        inp['price'] = jax.random.uniform(next(ks), (B, 1), dtype=jnp.float32) * 100.0
        tab_names = ['emb_user', 'emb_item', 'emb_age', 'emb_gender', 'emb_city', 'emb_category', 'emb_brand', 'emb_hour', 'emb_device']
        for name, v, d in zip(tab_names, VOCABS, EMB_DIMS):
            inp[name] = jax.random.normal(next(ks), (v, d), dtype=jnp.float32) * 0.05
        inp['w_dense'] = jax.random.normal(next(ks), (NUM_FEATURES,), dtype=jnp.float32) * 0.01
        inp['b_dense'] = jnp.zeros((), dtype=jnp.float32)
        inp['fm_v'] = jax.random.normal(next(ks), (NUM_FEATURES, E), dtype=jnp.float32) * 0.01
        dims = [DEEP_IN] + HIDDEN
        for i in range(len(HIDDEN)):
            inp[f'W{i + 1}'] = jax.random.normal(next(ks), (dims[i], dims[i + 1]), dtype=jnp.float32) * (1.0 / np.sqrt(dims[i]))
            inp[f'b{i + 1}'] = jnp.zeros((dims[i + 1],), dtype=jnp.float32)
        inp['Wo'] = jax.random.normal(next(ks), (HIDDEN[-1], 1), dtype=jnp.float32) * (1.0 / np.sqrt(HIDDEN[-1]))
        inp['bo'] = jnp.zeros((1,), dtype=jnp.float32)
        return inp
    _L0_rec_all = _L0_rec_setup()
    _L0_rec_in = {k: v for k, v in _L0_rec_all.items() if k in ('emb_user', 'emb_item', 'emb_age', 'emb_gender', 'emb_city', 'emb_category', 'emb_brand', 'emb_hour', 'emb_device', 'w_dense', 'b_dense', 'fm_v', 'W1', 'b1', 'W2', 'b2', 'W3', 'b3', 'Wo', 'bo')}
    del _L0_rec_all
    return {'r_price': r_price, 'r_user_id': r_user_id, 'r_item_id': r_item_id, 'r_age': r_age, 'r_gender': r_gender, 'r_city': r_city, 'r_category': r_category, 'r_brand': r_brand, 'r_hour': r_hour, 'r_device': r_device, 'L0_rec_emb_user': _L0_rec_in['emb_user'], 'L0_rec_emb_item': _L0_rec_in['emb_item'], 'L0_rec_emb_age': _L0_rec_in['emb_age'], 'L0_rec_emb_gender': _L0_rec_in['emb_gender'], 'L0_rec_emb_city': _L0_rec_in['emb_city'], 'L0_rec_emb_category': _L0_rec_in['emb_category'], 'L0_rec_emb_brand': _L0_rec_in['emb_brand'], 'L0_rec_emb_hour': _L0_rec_in['emb_hour'], 'L0_rec_emb_device': _L0_rec_in['emb_device'], 'L0_rec_w_dense': _L0_rec_in['w_dense'], 'L0_rec_b_dense': _L0_rec_in['b_dense'], 'L0_rec_fm_v': _L0_rec_in['fm_v'], 'L0_rec_W1': _L0_rec_in['W1'], 'L0_rec_b1': _L0_rec_in['b1'], 'L0_rec_W2': _L0_rec_in['W2'], 'L0_rec_b2': _L0_rec_in['b2'], 'L0_rec_W3': _L0_rec_in['W3'], 'L0_rec_b3': _L0_rec_in['b3'], 'L0_rec_Wo': _L0_rec_in['Wo'], 'L0_rec_bo': _L0_rec_in['bo']}

def reference(r_price, r_user_id, r_item_id, r_age, r_gender, r_city, r_category, r_brand, r_hour, r_device, L0_rec_emb_user, L0_rec_emb_item, L0_rec_emb_age, L0_rec_emb_gender, L0_rec_emb_city, L0_rec_emb_category, L0_rec_emb_brand, L0_rec_emb_hour, L0_rec_emb_device, L0_rec_w_dense, L0_rec_b_dense, L0_rec_fm_v, L0_rec_W1, L0_rec_b1, L0_rec_W2, L0_rec_b2, L0_rec_W3, L0_rec_b3, L0_rec_Wo, L0_rec_bo):
    import jax
    import jax.numpy as jnp

    def _L0_rec_ref(user_id, item_id, age, gender, city, category, brand, price, hour, device, emb_user, emb_item, emb_age, emb_gender, emb_city, emb_category, emb_brand, emb_hour, emb_device, w_dense, b_dense, fm_v, W1, b1, W2, b2, W3, b3, Wo, bo):
        import jax, jax.numpy as jnp
        import numpy as np
        B = 256
        VOCABS = [12500, 6250, 10, 3, 100, 50, 1000, 24, 5]
        E = 16
        EMB_DIMS = [E, E, E // 2, E // 4, E // 2, E // 2, E // 2, E // 4, E // 4]
        NUM_FEATURES = sum(VOCABS) + 1
        DEEP_IN = sum(EMB_DIMS) + 1
        HIDDEN = [256, 128, 64]
        b = user_id.shape[0]
        rows = jnp.arange(b)
        ids = [user_id, item_id, age, gender, city, category, brand, hour, device]
        feat = jnp.zeros((b, NUM_FEATURES), dtype=price.dtype)
        off = 0
        for idx, v in zip(ids, VOCABS):
            feat = feat.at[rows, off + idx[:, 0]].set(1.0)
            off += v
        feat = feat.at[:, NUM_FEATURES - 1].set(price[:, 0] / 1000.0)
        logit_dense = feat @ w_dense + b_dense
        square_of_sum = jnp.square(feat @ fm_v)
        sum_of_square = jnp.square(feat) @ jnp.square(fm_v)
        logit_fm = 0.5 * jnp.sum(square_of_sum - sum_of_square, axis=1)
        tables = [emb_user, emb_item, emb_age, emb_gender, emb_city, emb_category, emb_brand, emb_hour, emb_device]
        embs = [t[i[:, 0]] for t, i in zip(tables, ids)]
        deep_in = jnp.concatenate(embs + [price], axis=1)
        h = jax.nn.relu(deep_in @ W1 + b1)
        h = jax.nn.relu(h @ W2 + b2)
        h = jax.nn.relu(h @ W3 + b3)
        logit_deep = (h @ Wo + bo)[:, 0]
        return logit_dense + logit_fm + logit_deep
    y = _L0_rec_ref(r_user_id, r_item_id, r_age, r_gender, r_city, r_category, r_brand, r_price, r_hour, r_device, L0_rec_emb_user, L0_rec_emb_item, L0_rec_emb_age, L0_rec_emb_gender, L0_rec_emb_city, L0_rec_emb_category, L0_rec_emb_brand, L0_rec_emb_hour, L0_rec_emb_device, L0_rec_w_dense, L0_rec_b_dense, L0_rec_fm_v, L0_rec_W1, L0_rec_b1, L0_rec_W2, L0_rec_b2, L0_rec_W3, L0_rec_b3, L0_rec_Wo, L0_rec_bo)
    return y

_drawn_inputs = setup_inputs


def setup_inputs(seed=0):
    import zlib

    import numpy as np

    out = dict(_drawn_inputs(seed))
    spreads = {'L0_rec_b1': (0.0, 0.8), 'L0_rec_b2': (0.0, 0.446), 'L0_rec_b3': (0.0, 2.0)}
    factors = {'L0_rec_emb_user': 8.0,
     'L0_rec_emb_item': 8.0,
     'L0_rec_emb_age': 23.062,
     'L0_rec_emb_gender': 8.0,
     'L0_rec_emb_city': 23.691,
     'L0_rec_emb_category': 8.0,
     'L0_rec_emb_brand': 25.304,
     'L0_rec_emb_hour': 21.375,
     'L0_rec_emb_device': 31.116,
     'L0_rec_w_dense': 9.699,
     'L0_rec_fm_v': 8.0,
     'L0_rec_W3': 3.055}
    for name, (base, spread) in spreads.items():
        noise = np.random.default_rng([zlib.crc32(name.encode()), seed]).standard_normal(out[name].shape)
        drawn = base * np.exp(spread * noise) if base else spread * noise
        out[name] = jnp.asarray(drawn.astype(out[name].dtype))
    for name, factor in factors.items():
        out[name] = (out[name] * factor).astype(out[name].dtype)
    return out
```

```python
import numpy as np
import concourse.bass as bass
from concourse import mybir
from contextlib import ExitStack

P = 128
BATCH = 2048
TILES = BATCH // P
NAMES = ["user", "item", "age", "gender", "city", "category", "brand", "hour", "device"]
VOCABS = [12500, 6250, 10, 3, 100, 50, 1000, 24, 5]
DIMS = [16, 16, 8, 4, 8, 8, 8, 4, 4]
E = 16
NFEAT = len(NAMES)
NF = sum(VOCABS) + 1
OFFSET = [sum(VOCABS[:i]) for i in range(NFEAT)]
REC = 2 * E + 1
BRAND = NAMES.index("brand")
SMALL = [f for f in range(2, NFEAT) if f != BRAND]
SLOT_FEATS = SMALL + [BRAND]
SMALL_EMB = sum(DIMS[f] for f in SMALL)
SMALL_COLS = SMALL_EMB + E + 1
CHUNK_A = [NAMES.index("city"), NAMES.index("hour")]
CHUNK_B = [NAMES.index("category"), NAMES.index("age"), NAMES.index("gender"), NAMES.index("device")]
BRAND_DIM = DIMS[BRAND]
BRAND_COLS = BRAND_DIM + E + 1
BLOCK = 8
BLOCK_SHIFT = 3
TAB_COLS = 2 * SMALL_COLS + BLOCK * BRAND_COLS
COL_SMALL = 2 * E
COL_PRICE = COL_SMALL + SMALL_EMB
COL_BRAND = COL_PRICE + 1
DEEP = COL_BRAND + BRAND_DIM
Z_COLS = DEEP + E + 1
H1, H2, H3 = 256, 128, 64
PAIR = 2
GROUPS = TILES // PAIR
GN = PAIR * P
OH_BLOCK = 512
C_OFF = 0
C_VOC = C_OFF + NFEAT
C_IOTA = C_VOC + NFEAT
C_SLOTV = C_IOTA + BLOCK
C_SLOTV1 = C_SLOTV + 1
C_CMP = C_SLOTV1 + 1
C_COLS = C_CMP + 3
PB1, PB2, PB3, PWO, P_COLS = 0, 2, 3, 4, 5


def rec_kernel(nc, ids_tok, ids_slot, price, user_rec, item_rec, tables, last_row, w1, w2, w3, params, consts,
               scratch, out):
    fp32, bf16, fp16, i32 = mybir.dt.float32, mybir.dt.bfloat16, mybir.dt.float16, mybir.dt.int32
    ALU = mybir.AluOpType
    ACT = mybir.ActivationFunctionType
    AX = mybir.AxisListType.X
    NS = len(SLOT_FEATS)

    with ExitStack() as ctx:
        def sb(name, shape, dt=fp32):
            return ctx.enter_context(nc.sbuf_tensor(name, shape, dt))

        def ps(name, shape):
            return ctx.enter_context(nc.psum_tensor(name, shape, fp32))

        def sem(name):
            return ctx.enter_context(nc.semaphore(name))

        ids = sb("ids", [P, NFEAT, TILES], i32)
        slot_ids = sb("slot_ids", [NS * TILES, P], i32)
        pr = sb("pr", [P, TILES])
        tab = sb("tab", [P, TAB_COLS])
        lastb = sb("lastb", [P, E + 3])
        w1s = sb("w1s", [DEEP, H1])
        w2s = sb("w2s", [P, 2, H2])
        w3s = sb("w3s", [P, H3])
        par = sb("par", [P, P_COLS])
        cst = sb("cst", [P, C_COLS])
        ident = sb("ident", [P, P])
        ones = sb("ones", [P, 1])
        pq = sb("pq", [P, NFEAT, TILES])
        idx = sb("idx", [P, NFEAT, TILES], i32)
        wrap = sb("wrap", [P, NFEAT, TILES])
        pos = sb("pos", [P, NFEAT, TILES])
        low_ok = sb("low_ok", [P, NFEAT, TILES])
        valid = sb("valid", [P, NFEAT, TILES])
        same = sb("same", [P, NFEAT - 1, NFEAT - 1, TILES])
        dup = sb("dup", [P, NFEAT - 1, TILES])
        kept = sb("kept", [P, TILES, 2])
        rows = sb("rows", [P, TILES, 2, REC])
        bneg = sb("bneg", [P, TILES])
        bsum = sb("bsum", [P, TILES])
        bclip = sb("bclip", [P, TILES], i32)
        blow = sb("blow", [P, TILES], i32)
        bmask = sb("bmask", [P, TILES, BLOCK])
        below = sb("below", [P, NFEAT - 2, TILES])
        above = sb("above", [P, NFEAT - 2, TILES])
        outside = sb("outside", [P, NFEAT - 2, TILES])
        anyout = sb("anyout", [P, 1])
        flag = sb("flag", [1, 1], i32)
        sneg = sb("sneg", [NS * TILES, P])
        ssum = sb("ssum", [NS * TILES, P])
        sclip = sb("sclip", [NS * TILES, P], i32)
        s16 = sb("s16", [NS * TILES, P], fp16)
        idrow = [sb(f"idrow{c}", [P, BATCH], fp16) for c in range(3)]
        hot = [sb(f"hot{c}", [P, BATCH], bf16) for c in range(3)]
        tsq = sb("tsq", [P, 2 + BLOCK, E])
        tsum = sb("tsum", [P, 2 + BLOCK])
        part = [sb(f"part{k}", [P, TAB_COLS], bf16) for k in range(3)]
        rest = [sb(f"rest{k}", [P, TAB_COLS]) for k in range(2)]
        prs = sb("prs", [P, TILES])
        prsq = sb("prsq", [P, TILES])
        prq = sb("prq", [P, TILES])
        vlsq = sb("vlsq", [P, E])
        vlq = sb("vlq", [P, 1])
        bsc = sb("bsc", [P, 1])
        base = sb("base", [P, TILES, E + 1])
        Z = sb("Z", [P, TILES, Z_COLS])
        XT = sb("XT", [DEEP, BATCH])
        h1 = sb("h1", [P, 2, BATCH])
        h2 = sb("h2", [P, BATCH])
        h3 = sb("h3", [H3, BATCH])
        bprod = sb("bprod", [P, 2, PAIR, BLOCK, BRAND_COLS])
        front = sb("front", [P, TILES, E + 1])
        wrows = sb("wrows", [P, TILES, 2, E + 1])
        rsq = sb("rsq", [P, TILES, 2, E])
        rq = sb("rq", [P, TILES])
        S = sb("S", [P, TILES, E + 1])
        ssq = sb("ssq", [P, TILES, E])
        sq = sb("sq", [P, TILES])
        fm = sb("fm", [P, TILES])
        y = sb("y", [P, TILES])
        gkept = sb("gkept", [P, TILES, NFEAT])
        gidx = sb("gidx", [P, NFEAT], i32)
        grow = sb("grow", [P, NFEAT, REC])
        gw = sb("gw", [P, NFEAT, E + 1])
        gsq = sb("gsq", [P, NFEAT, E])
        gq = sb("gq", [P, 1])
        gsum = sb("gsum", [P, 1, E + 1])
        gsumsq = sb("gsumsq", [P, E])
        gs = sb("gs", [P, 1])

        psF = [ps(f"psF{i}", [P, 512]) for i in range(2)]
        psX = ps("psX", [P, 512])
        psH1 = [ps(f"psH1{c}", [P, 512]) for c in range(2)]
        psH2 = ps("psH2", [P, 512])
        psH3 = ps("psH3", [P, 512])
        psY = ps("psY", [P, 512])
        psFlag = psX[0:1, 511:512]

        def brand_ps(g):
            return psF[g % 2][:, 0:PAIR * BLOCK * BRAND_COLS]

        def small_ps(g):
            o = PAIR * BLOCK * BRAND_COLS
            return psF[g % 2][:, o:o + PAIR * SMALL_COLS].rearrange("p (t c) -> p t c", t=PAIR)

        ids_in = sem("ids_in")
        slots_in = sem("slots_in")
        cst_in = sem("cst_in")
        price_in = sem("price_in")
        tab_in = sem("tab_in")
        last_in = sem("last_in")
        w_in = sem("w_in")
        par_in = sem("par_in")
        dve_done = sem("dve_done")
        idx_ready = sem("idx_ready")
        s16_ready = sem("s16_ready")
        scratch_ready = sem("scratch_ready")
        idrow_in = [sem(f"idrow_in{c}") for c in range(3)]
        hot_ready = sem("hot_ready")
        tab_ready = sem("tab_ready")
        ident0 = sem("ident0")
        ident_ready = sem("ident_ready")
        ones_ready = sem("ones_ready")
        anyout_ready = sem("anyout_ready")
        flag_sum = sem("flag_sum")
        flag_ready = sem("flag_ready")
        zprice_ready = sem("zprice_ready")
        rows_in = [sem(f"rows_in{g}") for g in range(GROUPS)]
        front_done = sem("front_done")
        brand_ready = sem("brand_ready")
        front_read = sem("front_read")
        small_read = sem("small_read")
        zrows_ready = sem("zrows_ready")
        xt_done = sem("xt_done")
        xt_ready = sem("xt_ready")
        h1_done = sem("h1_done")
        h1a_ready = sem("h1a_ready")
        h1b_ready = sem("h1b_ready")
        h2_done = sem("h2_done")
        h2_ready = sem("h2_ready")
        h3_done = sem("h3_done")
        h3_ready = sem("h3_ready")
        deep_done = sem("deep_done")
        gidx_ready = sem("gidx_ready")
        grow_in = sem("grow_in")
        pool_turn = sem("pool_turn")
        gdve_done = sem("gdve_done")
        y_ready = sem("y_ready")
        out_done = sem("out_done")

        block = ctx.enter_context(nc.Block())

        @block.sync
        def _(sp):
            sp.dma_start(ids[:, :, :], ids_tok).then_inc(ids_in, 16)
            sp.dma_start(cst[:, :], consts).then_inc(cst_in, 16)
            sp.dma_start(tab[:, :], tables).then_inc(tab_in, 16)
            sp.wait_ge(s16_ready, 1)
            sp.dma_start(scratch.rearrange("f (t p) -> (f t) p", p=P), s16[:, :]).then_inc(scratch_ready, 16)
            sp.wait_ge(scratch_ready, 16)
            for c, feats in ((0, CHUNK_A), (1, CHUNK_B)):
                at = 0
                for f in feats:
                    s = SLOT_FEATS.index(f)
                    sp.dma_start(idrow[c][at:at + VOCABS[f], :],
                                 scratch[s:s + 1, :].to_broadcast([VOCABS[f], BATCH])).then_inc(idrow_in[c], 16)
                    at += VOCABS[f]
            sp.dma_start(w3s[:, :], w3).then_inc(w_in, 16)
            sp.wait_ge(y_ready, 1)
            sp.dma_start(out.rearrange("(p t) -> p t", t=TILES), y[:, :]).then_inc(out_done, 16)
            sp.wait_ge(out_done, 16)

        @block.gpsimd
        def _(pool):
            nc.gpsimd.memset(ident[:, :], 0.0).then_inc(ident0, 1)
            nc.gpsimd.memset(ones[:, :], 1.0).then_inc(ones_ready, 1)
            pool.wait_ge(ident0, 1)
            nc.gpsimd.affine_select(out=ident[:, :], in_=ident[:, :], compare_op=ALU.not_equal, fill=1.0, base=0,
                                    pattern=[[-1, P]], channel_multiplier=1).then_inc(ident_ready, 1)
            pool.wait_ge(idx_ready, 1)
            for t in range(TILES):
                for f, table in ((0, user_rec), (1, item_rec)):
                    pool.indirect_dma_start(
                        out=rows[:, t, f, :], out_offset=None, in_=table,
                        in_offset=bass.IndirectOffsetOnAxis(ap=idx[:, f, t:t + 1], axis=0),
                    ).then_inc(rows_in[t // PAIR], 16)
            pool.wait_ge(flag_ready, 1)
            outside_found = pool.value_load(flag[0:1, 0:1])
            with pool.If(outside_found > 0):
                with pool.Fori(0, TILES) as t:
                    pool.wait_ge(gidx_ready, t + 1)
                    pool.sem_inc(pool_turn, 1)
                    for f in range(NFEAT):
                        pool.indirect_dma_start(
                            out=grow[:, f, :], out_offset=None, in_=user_rec,
                            in_offset=bass.IndirectOffsetOnAxis(ap=gidx[:, f:f + 1], axis=0),
                        ).then_inc(grow_in, 16)

        @block.scalar
        def _(act):
            act.dma_start(slot_ids[:, :], ids_slot).then_inc(slots_in, 16)
            act.dma_start(pr[:, :], price).then_inc(price_in, 16)
            act.dma_start(lastb[:, :], last_row.to_broadcast([P, E + 3])).then_inc(last_in, 16)
            act.dma_start(par[:, :], params).then_inc(par_in, 16)
            act.dma_start(w1s[:, :], w1).then_inc(w_in, 16)
            act.dma_start(w2s[:, :, :], w2.rearrange("(c k) n -> k c n", k=P)).then_inc(w_in, 16)
            act.wait_ge(scratch_ready, 16)
            s = SLOT_FEATS.index(BRAND)
            act.dma_start(idrow[2][:, :], scratch[s:s + 1, :].to_broadcast([P, BATCH])).then_inc(idrow_in[2], 16)
            act.wait_ge(price_in, 16)
            nc.scalar.copy(Z[:, :, COL_PRICE], pr[:, :]).then_inc(zprice_ready, 1)
            act.wait_ge(par_in, 16)

            def small_embeddings(g):
                act.wait_ge(front_read, g + 1)
                nc.scalar.copy(Z[:, g * PAIR:(g + 1) * PAIR, COL_SMALL:COL_PRICE],
                               small_ps(g)[:, :, 0:SMALL_EMB]).then_inc(small_read, 1)

            def row_embeddings(g):
                act.wait_ge(rows_in[g], PAIR * 2 * 16)
                nc.scalar.copy(Z[:, g * PAIR:(g + 1) * PAIR, 0:2 * E].rearrange("p t (f e) -> p t f e", f=2),
                               rows[:, g * PAIR:(g + 1) * PAIR, :, E + 1:REC]).then_inc(zrows_ready, 1)

            def xt_copy(g):
                act.wait_ge(xt_done, g + 1)
                nc.scalar.copy(XT[:, g * GN:(g + 1) * GN], psX[0:DEEP, 0:GN]).then_inc(xt_ready, 1)

            def h1a(g):
                act.wait_ge(h1_done, 2 * g + 1)
                nc.scalar.activation(h1[:, 0, g * GN:(g + 1) * GN], psH1[0][:, 0:GN], ACT.Relu,
                                     bias=par[:, PB1:PB1 + 1]).then_inc(h1a_ready, 1)

            def h2_relu(g):
                act.wait_ge(h2_done, g + 1)
                nc.scalar.activation(h2[:, g * GN:(g + 1) * GN], psH2[:, 0:GN], ACT.Relu,
                                     bias=par[:, PB2:PB2 + 1]).then_inc(h2_ready, 1)

            def h3_relu(g):
                act.wait_ge(h3_done, g + 1)
                nc.scalar.activation(h3[:, g * GN:(g + 1) * GN], psH3[0:H3, 0:GN], ACT.Relu,
                                     bias=par[0:H3, PB3:PB3 + 1]).then_inc(h3_ready, 1)

            small_embeddings(0)
            for g in range(GROUPS + 1):
                if g < GROUPS:
                    row_embeddings(g)
                    xt_copy(g)
                if g >= 1:
                    h2_relu(g - 1)
                if g < GROUPS:
                    h1a(g)
                if g >= 1:
                    h3_relu(g - 1)
                if g + 1 < GROUPS:
                    small_embeddings(g + 1)

        @block.vector
        def _(dve):
            done = [0]

            def mark(ins):
                ins.then_inc(dve_done, 1)
                done[0] += 1
                return done[0]

            def bt(ap, n):
                return ap.unsqueeze(2).to_broadcast([ap.shape[0], ap.shape[1], n])

            dve.wait_ge(ids_in, 16)
            dve.wait_ge(cst_in, 16)
            m = mark(nc.vector.tensor_tensor(pq[:, :, :], ids[:, :, :], bt(cst[:, C_OFF:C_OFF + NFEAT], TILES), ALU.add))
            dve.wait_ge(dve_done, m)
            nc.vector.tensor_scalar(idx[:, :, :], pq[:, :, :], 0.0, float(2 * NF - 1), ALU.max, ALU.min)\
                .then_inc(idx_ready, 1)

            nslot = NS * TILES
            dve.wait_ge(slots_in, 16)
            m = mark(nc.vector.tensor_scalar(sneg[:, :], slot_ids[:, :], 0.0, cst[0:nslot, C_SLOTV:C_SLOTV + 1],
                                             ALU.is_lt, ALU.mult))
            dve.wait_ge(dve_done, m)
            m = mark(nc.vector.tensor_tensor(ssum[:, :], sneg[:, :], slot_ids[:, :], ALU.add))
            dve.wait_ge(dve_done, m)
            m = mark(nc.vector.tensor_scalar(sclip[:, :], ssum[:, :], 0.0, cst[0:nslot, C_SLOTV1:C_SLOTV1 + 1],
                                             ALU.max, ALU.min))
            dve.wait_ge(dve_done, m)
            b0 = (NS - 1) * TILES
            m = mark(nc.vector.tensor_scalar(sclip[b0:nslot, :], sclip[b0:nslot, :], BLOCK_SHIFT, None,
                                             ALU.arith_shift_right))
            dve.wait_ge(dve_done, m)
            nc.vector.tensor_copy(s16[:, :], sclip[:, :]).then_inc(s16_ready, 1)

            dve.wait_ge(tab_in, 16)
            small_tab = tab[:, 0:2 * SMALL_COLS].rearrange("p (a c) -> p a c", a=2)
            brand_tab = tab[:, 2 * SMALL_COLS:TAB_COLS].rearrange("p (a c) -> p a c", a=BLOCK)
            sv = small_tab[:, :, SMALL_EMB:SMALL_EMB + E]
            bv = brand_tab[:, :, BRAND_DIM:BRAND_DIM + E]
            mark(nc.vector.tensor_tensor(tsq[:, 0:2, :], sv, sv, ALU.mult))
            m = mark(nc.vector.tensor_tensor(tsq[:, 2:2 + BLOCK, :], bv, bv, ALU.mult))
            dve.wait_ge(dve_done, m)
            m = mark(nc.vector.reduce_sum(tsum[:, :], tsq[:, :, :], AX))
            dve.wait_ge(dve_done, m)
            sl = small_tab[:, :, SMALL_COLS - 1]
            bl = brand_tab[:, :, BRAND_COLS - 1]
            mark(nc.vector.scalar_tensor_tensor(out=sl, in0=tsum[:, 0:2], scalar=-0.5, in1=sl,
                                                op0=ALU.mult, op1=ALU.add))
            m = mark(nc.vector.scalar_tensor_tensor(out=bl, in0=tsum[:, 2:2 + BLOCK], scalar=-0.5, in1=bl,
                                                    op0=ALU.mult, op1=ALU.add))
            src = tab
            for k in range(3):
                dve.wait_ge(dve_done, m)
                if k == 2:
                    nc.vector.tensor_copy(part[k][:, :], src[:, :]).then_inc(tab_ready, 1)
                    break
                m = mark(nc.vector.tensor_copy(part[k][:, :], src[:, :]))
                dve.wait_ge(dve_done, m)
                m = mark(nc.vector.tensor_tensor(rest[k][:, :], src[:, :], part[k][:, :], ALU.subtract))
                src = rest[k]

            bid = ids[:, BRAND, :]
            m = mark(nc.vector.tensor_scalar(bneg[:, :], bid, 0.0, float(VOCABS[BRAND]), ALU.is_lt, ALU.mult))
            dve.wait_ge(dve_done, m)
            m = mark(nc.vector.tensor_tensor(bsum[:, :], bneg[:, :], bid, ALU.add))
            dve.wait_ge(dve_done, m)
            m = mark(nc.vector.tensor_scalar(bclip[:, :], bsum[:, :], 0.0, float(VOCABS[BRAND] - 1), ALU.max, ALU.min))
            dve.wait_ge(dve_done, m)
            m = mark(nc.vector.tensor_scalar(blow[:, :], bclip[:, :], BLOCK - 1, None, ALU.bitwise_and))
            dve.wait_ge(dve_done, m)
            mask_m = mark(nc.vector.tensor_tensor(
                bmask[:, :, :], bt(blow[:, :], BLOCK),
                cst[:, C_IOTA:C_IOTA + BLOCK].unsqueeze(1).to_broadcast([P, TILES, BLOCK]), ALU.is_equal))

            mark(nc.vector.tensor_scalar(wrap[:, :, :], pq[:, :, :], float(NF), float(-NF), ALU.is_ge, ALU.mult))
            small_ids = ids[:, 2:NFEAT, :]
            mark(nc.vector.tensor_scalar(below[:, :, :], small_ids, 0.0, None, ALU.is_lt))
            m = mark(nc.vector.tensor_tensor(above[:, :, :], small_ids, bt(cst[:, C_VOC + 2:C_VOC + NFEAT], TILES),
                                             ALU.is_ge))
            dve.wait_ge(dve_done, m)
            mark(nc.vector.tensor_tensor(pos[:, :, :], pq[:, :, :], wrap[:, :, :], ALU.add))
            m = mark(nc.vector.tensor_tensor(outside[:, :, :], below[:, :, :], above[:, :, :], ALU.max))
            dve.wait_ge(dve_done, m)
            nc.vector.reduce_max(anyout[:, :], outside[:, :, :].rearrange("p f t -> p (f t)"), AX)\
                .then_inc(anyout_ready, 1)
            mark(nc.vector.tensor_scalar(low_ok[:, :, :], pos[:, :, :], 0.0, None, ALU.is_ge))

            def compare(f):
                n = NFEAT - 1 - f
                return mark(nc.vector.tensor_tensor(same[:, f, 0:n, :], pos[:, f + 1:NFEAT, :],
                                                    pos[:, f:f + 1, :].to_broadcast([P, n, TILES]), ALU.is_equal))

            def duplicated(f):
                n = NFEAT - 1 - f
                return mark(nc.vector.reduce_max(dup[:, f, :], same[:, f, 0:n, :].rearrange("p g t -> p t g"), AX))

            def weight(f):
                return mark(nc.vector.scalar_tensor_tensor(out=kept[:, :, f], in0=dup[:, f, :], scalar=0.0,
                                                           in1=valid[:, f, :], op0=ALU.is_equal, op1=ALU.mult))

            compare(0)
            m = compare(1)
            dve.wait_ge(dve_done, m)
            mark(nc.vector.scalar_tensor_tensor(out=valid[:, :, :], in0=pos[:, :, :], scalar=float(NF - 2),
                                                in1=low_ok[:, :, :], op0=ALU.is_le, op1=ALU.mult))
            duplicated(0)
            m = duplicated(1)
            dve.wait_ge(dve_done, m)
            weight(0)
            weight(1)

            dve.wait_ge(price_in, 16)
            dve.wait_ge(last_in, 16)
            vl = lastb[:, 0:E]
            mark(nc.vector.tensor_scalar(prs[:, :], pr[:, :], 0.001, None, ALU.mult))
            mark(nc.vector.tensor_tensor(vlsq[:, :], vl, vl, ALU.mult))
            m = mark(nc.vector.tensor_tensor(bsc[:, :], lastb[:, E + 1:E + 2], lastb[:, E + 2:E + 3], ALU.add))
            dve.wait_ge(dve_done, m)
            mark(nc.vector.tensor_tensor(base[:, :, :], bt(prs[:, :], E + 1),
                                         lastb[:, 0:E + 1].unsqueeze(1).to_broadcast([P, TILES, E + 1]), ALU.mult))
            mark(nc.vector.tensor_tensor(prsq[:, :], prs[:, :], prs[:, :], ALU.mult))
            m = mark(nc.vector.reduce_sum(vlq[:, :], vlsq[:, :], AX))
            dve.wait_ge(dve_done, m)
            m = mark(nc.vector.tensor_scalar(prq[:, :], prsq[:, :], vlq[:, 0:1], -0.5, ALU.mult, ALU.mult))
            dve.wait_ge(dve_done, m)
            base_m = mark(nc.vector.scalar_tensor_tensor(out=base[:, :, E], in0=prq[:, :], scalar=bsc[:, 0:1],
                                                         in1=base[:, :, E], op0=ALU.add, op1=ALU.add))

            for b in range(BATCH // OH_BLOCK):
                cols = slice(b * OH_BLOCK, (b + 1) * OH_BLOCK)
                for c, n in ((0, sum(VOCABS[f] for f in CHUNK_A)), (1, sum(VOCABS[f] for f in CHUNK_B)), (2, P)):
                    if b == 0:
                        dve.wait_ge(idrow_in[c], 16 * (len(CHUNK_A), len(CHUNK_B), 1)[c])
                    nc.vector.tensor_scalar(hot[c][0:n, cols], idrow[c][0:n, cols],
                                            cst[0:n, C_CMP + c:C_CMP + c + 1], None, ALU.is_equal)\
                        .then_inc(hot_ready, 1)

            dve.wait_ge(flag_sum, 1)
            nc.vector.tensor_copy(flag[:, :], psFlag).then_inc(flag_ready, 1)

            def brand_block(g):
                ts = slice(g * PAIR, (g + 1) * PAIR)
                dve.wait_ge(front_done, g + 1)
                prod = bprod[:, g % 2]
                mark(nc.vector.tensor_tensor(
                    prod.rearrange("p t j c -> p (t j) c"), brand_ps(g).rearrange("p (a c) -> p a c", c=BRAND_COLS),
                    bt(bmask[:, ts, :].rearrange("p t j -> p (t j)"), BRAND_COLS), ALU.mult))
                m = done[0]
                nc.vector.tensor_tensor(front[:, ts, :], small_ps(g)[:, :, SMALL_EMB:SMALL_COLS], base[:, ts, :],
                                        ALU.add).then_inc(front_read, 1)
                dve.wait_ge(dve_done, m)
                for t in range(PAIR):
                    nc.vector.reduce_sum(Z[:, g * PAIR + t, COL_BRAND:Z_COLS],
                                         prod[:, t].rearrange("p j c -> p c j"), AX).then_inc(brand_ready, 1)

            def h1b(g):
                dve.wait_ge(h1_done, 2 * g + 2)
                nc.vector.tensor_scalar(h1[:, 1, g * GN:(g + 1) * GN], psH1[1][:, 0:GN], par[:, PB1 + 1:PB1 + 2],
                                        0.0, ALU.add, ALU.max).then_inc(h1b_ready, 1)

            def machine(g):
                ts = slice(g * PAIR, (g + 1) * PAIR)
                dve.wait_ge(rows_in[g], PAIR * 2 * 16)
                w = wrows[:, ts].rearrange("p t f c -> p (t f) c")
                m = mark(nc.vector.tensor_tensor(
                    w, rows[:, ts, :, 0:E + 1].rearrange("p t f c -> p (t f) c"),
                    kept[:, ts, :].rearrange("p t f -> p (t f)").unsqueeze(2).to_broadcast([P, 2 * PAIR, E + 1]), ALU.mult))
                dve.wait_ge(dve_done, m)
                mark(nc.vector.tensor_tensor(rsq[:, ts].rearrange("p t f c -> p (t f) c"), w[:, :, 0:E], w[:, :, 0:E],
                                             ALU.mult))
                m = mark(nc.vector.tensor_tensor(S[:, ts, :], wrows[:, ts, 0, :], wrows[:, ts, 1, :], ALU.add))
                dve.wait_ge(dve_done, m)
                mark(nc.vector.reduce_sum(rq[:, ts], rsq[:, ts].rearrange("p t f c -> p t (f c)"), AX))
                m = mark(nc.vector.tensor_tensor(S[:, ts, :], S[:, ts, :], front[:, ts, :], ALU.add))
                dve.wait_ge(dve_done, m)
                m = mark(nc.vector.tensor_tensor(S[:, ts, :], S[:, ts, :], Z[:, ts, DEEP:Z_COLS], ALU.add))
                dve.wait_ge(dve_done, m)
                m = mark(nc.vector.tensor_tensor(ssq[:, ts, :], S[:, ts, 0:E], S[:, ts, 0:E], ALU.mult))
                dve.wait_ge(dve_done, m)
                m = mark(nc.vector.reduce_sum(sq[:, ts], ssq[:, ts, :], AX))
                dve.wait_ge(dve_done, m)
                m = mark(nc.vector.tensor_tensor(sq[:, ts], sq[:, ts], rq[:, ts], ALU.subtract))
                dve.wait_ge(dve_done, m)
                return mark(nc.vector.scalar_tensor_tensor(out=fm[:, ts], in0=sq[:, ts], scalar=0.5,
                                                           in1=S[:, ts, E], op0=ALU.mult, op1=ALU.add))

            brand_block(0)
            for g in range(GROUPS):
                if g + 1 < GROUPS:
                    brand_block(g + 1)
                h1b(g)
                m = machine(g)
            dve.wait_ge(dve_done, m)

            outside_found = dve.value_load(flag[0:1, 0:1])
            with dve.If(outside_found > 0):
                step = [0]

                def link(ins):
                    step[0] += 1
                    ins.then_inc(gdve_done, 1)
                    dve.wait_ge(gdve_done, step[0])

                for f in range(NFEAT - 1):
                    n = NFEAT - 1 - f
                    link(nc.vector.tensor_tensor(same[:, f, 0:n, :], pos[:, f + 1:NFEAT, :],
                                                 pos[:, f:f + 1, :].to_broadcast([P, n, TILES]), ALU.is_equal))
                    link(nc.vector.reduce_max(dup[:, f, :], same[:, f, 0:n, :].rearrange("p g t -> p t g"), AX))
                    link(nc.vector.scalar_tensor_tensor(out=gkept[:, :, f], in0=dup[:, f, :], scalar=0.0,
                                                        in1=valid[:, f, :], op0=ALU.is_equal, op1=ALU.mult))
                link(nc.vector.tensor_copy(gkept[:, :, NFEAT - 1], valid[:, NFEAT - 1, :]))
                before, steps = step[0], 10
                with dve.Fori(0, TILES) as t:
                    at = [before]

                    def chain(ins):
                        at[0] += 1
                        ins.then_inc(gdve_done, 1)
                        dve.wait_ge(gdve_done, t * steps + at[0])

                    chain(nc.vector.tensor_copy(gidx[:, :], idx[:, :, bass.ds(t, 1)].rearrange("p f a -> p (f a)")))
                    dve.sem_inc(gidx_ready, 1)
                    dve.wait_ge(grow_in, (t + 1) * (NFEAT * 16))
                    chain(nc.vector.tensor_tensor(
                        gw[:, :, :], grow[:, :, 0:E + 1],
                        gkept[:, bass.ds(t, 1), :].rearrange("p a f -> p (a f)").unsqueeze(2)
                        .to_broadcast([P, NFEAT, E + 1]), ALU.mult))
                    chain(nc.vector.tensor_tensor(gsq[:, :, :], gw[:, :, 0:E], gw[:, :, 0:E], ALU.mult))
                    chain(nc.vector.reduce_sum(gq[:, :], gsq[:, :, :].rearrange("p f c -> p (f c)"), AX))
                    chain(nc.vector.reduce_sum(gsum[:, 0, :], gw[:, :, :].rearrange("p f c -> p c f"), AX))
                    chain(nc.vector.tensor_tensor(gsum[:, :, :], gsum[:, :, :], base[:, bass.ds(t, 1), :], ALU.add))
                    chain(nc.vector.tensor_tensor(gsumsq[:, :], gsum[:, 0, 0:E], gsum[:, 0, 0:E], ALU.mult))
                    chain(nc.vector.reduce_sum(gs[:, :], gsumsq[:, :], AX))
                    chain(nc.vector.tensor_tensor(gs[:, :], gs[:, :], gq[:, :], ALU.subtract))
                    chain(nc.vector.scalar_tensor_tensor(out=fm[:, bass.ds(t, 1)], in0=gs[:, :], scalar=0.5,
                                                         in1=gsum[:, 0, E:E + 1], op0=ALU.mult, op1=ALU.add))
                    assert at[0] - before == steps

            dve.wait_ge(deep_done, GROUPS)
            nc.vector.tensor_tensor(y[:, :], psY[:, 0:TILES], fm[:, :], ALU.add).then_inc(y_ready, 1)

        @block.tensor
        def _(pe):
            pe.wait_ge(ones_ready, 1)
            pe.wait_ge(anyout_ready, 1)
            nc.tensor.matmul(psFlag, anyout[:, :], ones[:, :], start=True, stop=True).then_inc(flag_sum, 1)

            def lookups(g):
                if g == 0:
                    pe.wait_ge(tab_ready, 1)
                if g >= 2:
                    pe.wait_ge(small_read, g - 1)
                pe.wait_ge(hot_ready, 3 * (g * GN // OH_BLOCK + 1))
                nA, nB = (sum(VOCABS[f] for f in c) for c in (CHUNK_A, CHUNK_B))
                width = BLOCK * BRAND_COLS
                for t in range(PAIR):
                    tok = slice((g * PAIR + t) * P, (g * PAIR + t + 1) * P)
                    for k in range(3):
                        nc.tensor.matmul(brand_ps(g)[:, t * width:(t + 1) * width], hot[2][:, tok],
                                         part[k][:, 2 * SMALL_COLS:TAB_COLS], start=(k == 0), stop=(k == 2))
                    for k in range(3):
                        nc.tensor.matmul(small_ps(g)[:, t, :], hot[0][0:nA, tok], part[k][0:nA, 0:SMALL_COLS],
                                         start=(k == 0), stop=False)
                    for k in range(3):
                        last = nc.tensor.matmul(small_ps(g)[:, t, :], hot[1][0:nB, tok],
                                                part[k][0:nB, SMALL_COLS:2 * SMALL_COLS], start=False, stop=(k == 2))
                last.then_inc(front_done, 1)

            def transposes(g):
                pe.wait_ge(brand_ready, PAIR * (g + 1))
                pe.wait_ge(small_read, g + 1)
                pe.wait_ge(zrows_ready, g + 1)
                if g >= 1:
                    pe.wait_ge(xt_ready, g)
                for t in range(PAIR):
                    last = nc.tensor.transpose(psX[0:DEEP, t * P:(t + 1) * P], Z[:, g * PAIR + t, 0:DEEP], ident[:, :])
                last.then_inc(xt_done, 1)

            def layer1(g):
                if g >= 1:
                    pe.wait_ge(h1a_ready, g)
                    pe.wait_ge(h1b_ready, g)
                pe.wait_ge(xt_ready, g + 1)
                for c in range(2):
                    nc.tensor.matmul(psH1[c][:, 0:GN], w1s[:, c * P:(c + 1) * P], XT[:, g * GN:(g + 1) * GN],
                                     start=True, stop=True).then_inc(h1_done, 1)

            def layer2(g):
                if g >= 1:
                    pe.wait_ge(h2_ready, g)
                pe.wait_ge(h1a_ready, g + 1)
                nc.tensor.matmul(psH2[:, 0:GN], w2s[:, 0, :], h1[:, 0, g * GN:(g + 1) * GN], start=True, stop=False)
                pe.wait_ge(h1b_ready, g + 1)
                nc.tensor.matmul(psH2[:, 0:GN], w2s[:, 1, :], h1[:, 1, g * GN:(g + 1) * GN], start=False, stop=True)\
                    .then_inc(h2_done, 1)

            def layer3(g):
                if g >= 1:
                    pe.wait_ge(h3_ready, g)
                pe.wait_ge(h2_ready, g + 1)
                nc.tensor.matmul(psH3[0:H3, 0:GN], w3s[:, :], h2[:, g * GN:(g + 1) * GN], start=True, stop=True)\
                    .then_inc(h3_done, 1)

            def layer4(g):
                pe.wait_ge(h3_ready, g + 1)
                for t in range(g * PAIR, (g + 1) * PAIR):
                    last = nc.tensor.matmul(psY[:, t:t + 1], h3[:, t * P:(t + 1) * P], par[0:H3, PWO:PWO + 1],
                                            start=True, stop=True)
                last.then_inc(deep_done, 1)

            lookups(0)
            pe.wait_ge(ident_ready, 1)
            pe.wait_ge(zprice_ready, 1)
            pe.wait_ge(flag_ready, 1)
            pe.wait_ge(w_in, 3 * 16)
            pe.wait_ge(par_in, 16)
            for g in range(GROUPS + 1):
                if g < GROUPS:
                    transposes(g)
                if g >= 1:
                    layer2(g - 1)
                if g < GROUPS:
                    layer1(g)
                if g >= 1:
                    layer3(g - 1)
                if g + 1 < GROUPS:
                    lookups(g + 1)
                if g >= 1:
                    layer4(g - 1)


def build(nc, arrays):
    args = {name: nc.dram_tensor(name, a.shape, mybir.dt.from_np(a.dtype), kind="ExternalInput").ap()
            for name, a in arrays.items()}
    scratch = nc.dram_tensor("slot_rows", (len(SLOT_FEATS), BATCH), mybir.dt.float16, kind="Internal").ap()
    out = nc.dram_tensor("out", (BATCH,), mybir.dt.float32, kind="ExternalOutput").ap()
    rec_kernel(nc, scratch=scratch, out=out, **args)


def edge(table, before, after):
    return np.concatenate([np.repeat(table[:1], before, 0), table, np.repeat(table[-1:], after, 0)])


def constants():
    c = np.zeros((P, C_COLS), np.float32)
    for f in range(NFEAT):
        c[:, C_OFF + f] = OFFSET[f] + NF
        c[:, C_VOC + f] = VOCABS[f]
    c[:, C_IOTA:C_IOTA + BLOCK] = np.arange(BLOCK)
    for s, f in enumerate(SLOT_FEATS):
        c[s * TILES:(s + 1) * TILES, C_SLOTV] = VOCABS[f]
        c[s * TILES:(s + 1) * TILES, C_SLOTV1] = VOCABS[f] - 1
    for k, feats in enumerate((CHUNK_A, CHUNK_B)):
        at = 0
        for f in feats:
            c[at:at + VOCABS[f], C_CMP + k] = np.arange(VOCABS[f])
            at += VOCABS[f]
    c[:, C_CMP + 2] = np.arange(P)
    return c


def lay_out(inputs):
    x = {k: np.asarray(v) for k, v in inputs.items()}
    ids = np.stack([x[f"r_{n}_id"] if f"r_{n}_id" in x else x[f"r_{n}"] for n in NAMES])[:, :, 0]
    by_tile = ids.reshape(NFEAT, P, TILES)
    emb = [x[f"L0_rec_emb_{n}"] for n in NAMES]
    fm_v, w_dense = x["L0_rec_fm_v"], x["L0_rec_w_dense"][:, None]

    def records(f):
        v, o = VOCABS[f], OFFSET[f]
        rows = np.concatenate([edge(emb[f], NF + o - v, 0), edge(emb[f], 0, NF - o - v)])
        return np.concatenate([np.concatenate([fm_v, fm_v]), np.concatenate([w_dense, w_dense]), rows], 1)

    tables = np.zeros((P, TAB_COLS), np.float32)
    emb_at = {f: sum(DIMS[g] for g in SMALL[:i]) for i, f in enumerate(SMALL)}
    for k, feats in enumerate((CHUNK_A, CHUNK_B)):
        at, c0 = 0, k * SMALL_COLS
        for f in feats:
            rows = slice(at, at + VOCABS[f])
            here = slice(OFFSET[f], OFFSET[f] + VOCABS[f])
            tables[rows, c0 + emb_at[f]:c0 + emb_at[f] + DIMS[f]] = emb[f]
            tables[rows, c0 + SMALL_EMB:c0 + SMALL_EMB + E] = fm_v[here]
            tables[rows, c0 + SMALL_COLS - 1:c0 + SMALL_COLS] = w_dense[here]
            at += VOCABS[f]
    here = slice(OFFSET[BRAND], OFFSET[BRAND] + VOCABS[BRAND])
    brand = np.concatenate([emb[BRAND], fm_v[here], w_dense[here]], 1)
    tables[0:VOCABS[BRAND] // BLOCK, 2 * SMALL_COLS:] = brand.reshape(VOCABS[BRAND] // BLOCK, BLOCK * BRAND_COLS)

    w1_at = [sum(DIMS[:f]) for f in range(NFEAT + 1)]
    order = [0, 1] + SMALL + [NFEAT] + [BRAND]
    w1 = np.concatenate([x["L0_rec_W1"][w1_at[f]:w1_at[f] + (DIMS + [1])[f]] for f in order])
    params = np.zeros((P, P_COLS), np.float32)
    params[:, PB1:PB1 + 2] = x["L0_rec_b1"].reshape(2, P).T
    params[:, PB2] = x["L0_rec_b2"]
    params[0:H3, PB3] = x["L0_rec_b3"]
    params[0:H3, PWO] = x["L0_rec_Wo"][:, 0]
    return {
        "ids_tok": np.ascontiguousarray(by_tile.transpose(1, 0, 2)),
        "ids_slot": np.ascontiguousarray(by_tile[SLOT_FEATS].transpose(0, 2, 1)).reshape(-1, P),
        "price": x["r_price"].reshape(P, TILES),
        "user_rec": records(0),
        "item_rec": records(1),
        "tables": tables,
        "last_row": np.concatenate([fm_v[-1], w_dense[-1], x["L0_rec_b_dense"].reshape(1),
                                    x["L0_rec_bo"]]).reshape(1, -1),
        "w1": w1,
        "w2": x["L0_rec_W2"],
        "w3": x["L0_rec_W3"],
        "params": params,
        "consts": constants(),
    }


def kernel(**inputs):
    import concourse.bacc as _bacc
    from concourse.bass_utils import run_bass_kernel_spmd as _run

    nc = _bacc.Bacc("TRN2", target_bir_lowering=False, num_devices=1)
    arrays = lay_out(inputs)
    build(nc, arrays)
    r = _run(nc, [arrays], core_ids=[0])
    return r.results[0]["out"]
```

```python
import numpy as np
import concourse.bass as bass
from concourse import mybir
from contextlib import ExitStack

P = 128
BATCH = 2048
TILES = BATCH // P
NAMES = ["user", "item", "age", "gender", "city", "category", "brand", "hour", "device"]
VOCABS = [12500, 6250, 10, 3, 100, 50, 1000, 24, 5]
DIMS = [16, 16, 8, 4, 8, 8, 8, 4, 4]
E = 16
NFEAT = len(NAMES)
NF = sum(VOCABS) + 1
OFFSET = [sum(VOCABS[:i]) for i in range(NFEAT)]
REC = 2 * E + 1
BRAND = NAMES.index("brand")
SMALL = [f for f in range(2, NFEAT) if f != BRAND]
SLOT_FEATS = SMALL + [BRAND]
SMALL_EMB = sum(DIMS[f] for f in SMALL)
SMALL_COLS = SMALL_EMB + E + 1
CHUNK_A = [NAMES.index("city"), NAMES.index("hour")]
CHUNK_B = [NAMES.index("category"), NAMES.index("age"), NAMES.index("gender"), NAMES.index("device")]
BRAND_DIM = DIMS[BRAND]
BRAND_COLS = BRAND_DIM + E + 1
BLOCK = 8
BLOCK_SHIFT = 3
TAB_COLS = 2 * SMALL_COLS + BLOCK * BRAND_COLS
COL_SMALL = 2 * E
COL_PRICE = COL_SMALL + SMALL_EMB
COL_BRAND = COL_PRICE + 1
DEEP = COL_BRAND + BRAND_DIM
Z_COLS = DEEP + E + 1
H1, H2, H3 = 256, 128, 64
PAIR = 2
SIZES = [PAIR] * (TILES // PAIR - 1) + [1] * PAIR
STARTS = [sum(SIZES[:g]) for g in range(len(SIZES))]
GROUPS = len(SIZES)
OH_BLOCK = 512
C_OFF = 0
C_VOC = C_OFF + NFEAT
C_IOTA = C_VOC + NFEAT
C_SLOTV = C_IOTA + BLOCK
C_SLOTV1 = C_SLOTV + 1
C_CMP = C_SLOTV1 + 1
C_COLS = C_CMP + 3
PB1 = C_COLS
PB2, PB3, PWO = PB1 + 2, PB1 + 3, PB1 + 4
P_PRICE = PWO + 2
P_LAST = P_PRICE + TILES
FACTS = P_LAST + E + 3
INTS = NFEAT * TILES + P
W_COLS = H1 + 2 * H2 + H3


def rec_kernel(nc, ints, facts, user_rec, item_rec, tables, weights, scratch, out):
    fp32, bf16, fp16, i32 = mybir.dt.float32, mybir.dt.bfloat16, mybir.dt.float16, mybir.dt.int32
    ALU = mybir.AluOpType
    ACT = mybir.ActivationFunctionType
    AX = mybir.AxisListType.X
    NS = len(SLOT_FEATS)

    with ExitStack() as ctx:
        def sb(name, shape, dt=fp32):
            return ctx.enter_context(nc.sbuf_tensor(name, shape, dt))

        def ps(name, shape):
            return ctx.enter_context(nc.psum_tensor(name, shape, fp32))

        def sem(name):
            return ctx.enter_context(nc.semaphore(name))

        ints_sb = sb("ints_sb", [P, INTS], i32)
        ids = ints_sb[:, 0:NFEAT * TILES].rearrange("p (f t) -> p f t", f=NFEAT)
        slot_ids = ints_sb[0:NS * TILES, NFEAT * TILES:INTS]
        cst = par = sb("facts_sb", [P, FACTS])
        pr = cst[:, P_PRICE:P_LAST]
        lastb = cst[:, P_LAST:FACTS]
        w_sb = sb("w_sb", [P, W_COLS])
        w1s = w_sb[0:DEEP, 0:H1]
        w2s = w_sb[:, H1:H1 + 2 * H2].rearrange("p (c n) -> p c n", c=2)
        w3s = w_sb[:, H1 + 2 * H2:W_COLS]
        tab = sb("tab", [P, TAB_COLS])
        ident = sb("ident", [P, P])
        ones = sb("ones", [P, 1])
        pq = sb("pq", [P, NFEAT, TILES])
        idx = sb("idx", [P, NFEAT, TILES], i32)
        wrap = sb("wrap", [P, NFEAT, TILES])
        pos = sb("pos", [P, NFEAT, TILES])
        low_ok = sb("low_ok", [P, NFEAT, TILES])
        valid = sb("valid", [P, NFEAT, TILES])
        same = sb("same", [P, NFEAT - 1, NFEAT - 1, TILES])
        dup = sb("dup", [P, NFEAT - 1, TILES])
        kept = sb("kept", [P, TILES, 2])
        rows = sb("rows", [P, TILES, 2, REC])
        bneg = sb("bneg", [P, TILES])
        bsum = sb("bsum", [P, TILES])
        bclip = sb("bclip", [P, TILES], i32)
        blow = sb("blow", [P, TILES], i32)
        bmask = sb("bmask", [P, TILES, BLOCK])
        below = sb("below", [P, NFEAT - 2, TILES])
        above = sb("above", [P, NFEAT - 2, TILES])
        outside = sb("outside", [P, NFEAT - 2, TILES])
        anyout = sb("anyout", [P, 1])
        flag = sb("flag", [1, 1], i32)
        sneg = sb("sneg", [NS * TILES, P])
        ssum = sb("ssum", [NS * TILES, P])
        sclip = sb("sclip", [NS * TILES, P], i32)
        s16 = sb("s16", [NS * TILES, P], fp16)
        idrow = [sb(f"idrow{c}", [P, BATCH], fp16) for c in range(3)]
        hot = [sb(f"hot{c}", [P, BATCH], bf16) for c in range(3)]
        tsq = sb("tsq", [P, 2 + BLOCK, E])
        tsum = sb("tsum", [P, 2 + BLOCK])
        part = [sb(f"part{k}", [P, TAB_COLS], bf16) for k in range(3)]
        rest = [sb(f"rest{k}", [P, TAB_COLS]) for k in range(2)]
        prs = sb("prs", [P, TILES])
        prsq = sb("prsq", [P, TILES])
        prq = sb("prq", [P, TILES])
        vlsq = sb("vlsq", [P, E])
        vlq = sb("vlq", [P, 1])
        bsc = sb("bsc", [P, 1])
        base = sb("base", [P, TILES, E + 1])
        Z = sb("Z", [P, TILES, Z_COLS])
        XT = sb("XT", [DEEP, BATCH])
        h1 = sb("h1", [P, 2, BATCH])
        h2 = sb("h2", [P, BATCH])
        h3 = sb("h3", [2 * H3, GROUPS, P])
        bprod = sb("bprod", [P, 2, PAIR, BLOCK, BRAND_COLS])
        front = sb("front", [P, TILES, E + 1])
        wrows = sb("wrows", [P, TILES, 2, E + 1])
        rsq = sb("rsq", [P, TILES, 2, E])
        rq = sb("rq", [P, TILES])
        S = sb("S", [P, TILES, E + 1])
        ssq = sb("ssq", [P, TILES, E])
        sq = sb("sq", [P, TILES])
        fm = sb("fm", [P, TILES])
        y = sb("y", [P, TILES])
        gkept = sb("gkept", [P, TILES, NFEAT])
        gidx = sb("gidx", [P, NFEAT], i32)
        grow = sb("grow", [P, NFEAT, REC])
        gw = sb("gw", [P, NFEAT, E + 1])
        gsq = sb("gsq", [P, NFEAT, E])
        gq = sb("gq", [P, 1])
        gsum = sb("gsum", [P, 1, E + 1])
        gsumsq = sb("gsumsq", [P, E])
        gs = sb("gs", [P, 1])

        psF = [ps(f"psF{i}", [P, 512]) for i in range(2)]
        psX = ps("psX", [P, 512])
        psH1 = [ps(f"psH1{c}", [P, 512]) for c in range(2)]
        psH2 = ps("psH2", [P, 512])
        psH3 = ps("psH3", [P, 512])
        psY = ps("psY", [P, 512])
        psFlag = psY[0:1, 511:512]

        def tiles(g):
            return slice(STARTS[g], STARTS[g] + SIZES[g])

        def tokens(g):
            return slice(STARTS[g] * P, (STARTS[g] + SIZES[g]) * P)

        def brand_ps(g):
            return psF[g % 2][:, 0:SIZES[g] * BLOCK * BRAND_COLS]

        def small_ps(g):
            o = PAIR * BLOCK * BRAND_COLS
            return psF[g % 2][:, o:o + SIZES[g] * SMALL_COLS].rearrange("p (t c) -> p t c", t=SIZES[g])

        ints_in = sem("ints_in")
        facts_in = sem("facts_in")
        tab_in = sem("tab_in")
        w_in = sem("w_in")
        dve_done = sem("dve_done")
        idx_ready = sem("idx_ready")
        s16_ready = sem("s16_ready")
        scratch_ready = sem("scratch_ready")
        idrow_in = [sem(f"idrow_in{c}") for c in range(3)]
        hot_ready = sem("hot_ready")
        tab_ready = sem("tab_ready")
        ident0 = sem("ident0")
        ident_ready = sem("ident_ready")
        ones_ready = sem("ones_ready")
        anyout_ready = sem("anyout_ready")
        flag_sum = sem("flag_sum")
        flag_ready = sem("flag_ready")
        zprice_ready = sem("zprice_ready")
        rows_in = [sem(f"rows_in{g}") for g in range(GROUPS)]
        front_done = sem("front_done")
        brand_ready = sem("brand_ready")
        front_read = sem("front_read")
        small_read = sem("small_read")
        zrows_ready = sem("zrows_ready")
        xt_done = sem("xt_done")
        xt_ready = sem("xt_ready")
        h1_done = sem("h1_done")
        h1a_ready = sem("h1a_ready")
        h1b_ready = sem("h1b_ready")
        h2_done = sem("h2_done")
        h2_ready = sem("h2_ready")
        h3_done = sem("h3_done")
        h3_ready = sem("h3_ready")
        deep_done = sem("deep_done")
        gidx_ready = sem("gidx_ready")
        grow_in = sem("grow_in")
        pool_turn = sem("pool_turn")
        gdve_done = sem("gdve_done")
        y_ready = sem("y_ready")
        out_done = sem("out_done")

        block = ctx.enter_context(nc.Block())

        def spread(eng, feats):
            for f in feats:
                c = 0 if f in CHUNK_A else 1 if f in CHUNK_B else 2
                at = sum(VOCABS[g] for g in ((CHUNK_A, CHUNK_B)[c][:(CHUNK_A, CHUNK_B)[c].index(f)] if c < 2 else ()))
                n = P if c == 2 else VOCABS[f]
                s = SLOT_FEATS.index(f)
                eng.dma_start(idrow[c][at:at + n, :], scratch[s:s + 1, :].to_broadcast([n, BATCH]))\
                   .then_inc(idrow_in[c], 16)

        @block.sync
        def _(sp):
            sp.dma_start(ints_sb[:, :], ints).then_inc(ints_in, 16)
            sp.dma_start(tab[:, :], tables).then_inc(tab_in, 16)
            sp.wait_ge(s16_ready, 1)
            sp.dma_start(scratch.rearrange("f (t p) -> (f t) p", p=P), s16[:, :]).then_inc(scratch_ready, 16)
            sp.wait_ge(scratch_ready, 16)
            spread(sp, [BRAND] + CHUNK_B[:2])
            sp.wait_ge(y_ready, 1)
            sp.dma_start(out.rearrange("(p t) -> p t", t=TILES), y[:, :]).then_inc(out_done, 16)
            sp.wait_ge(out_done, 16)

        @block.gpsimd
        def _(pool):
            nc.gpsimd.memset(ident[:, :], 0.0).then_inc(ident0, 1)
            nc.gpsimd.memset(ones[:, :], 1.0).then_inc(ones_ready, 1)
            pool.wait_ge(ident0, 1)
            nc.gpsimd.affine_select(out=ident[:, :], in_=ident[:, :], compare_op=ALU.not_equal, fill=1.0, base=0,
                                    pattern=[[-1, P]], channel_multiplier=1).then_inc(ident_ready, 1)
            pool.wait_ge(idx_ready, 1)
            for g in range(GROUPS):
                for t in range(STARTS[g], STARTS[g] + SIZES[g]):
                    for f, table in ((0, user_rec), (1, item_rec)):
                        pool.indirect_dma_start(
                            out=rows[:, t, f, :], out_offset=None, in_=table,
                            in_offset=bass.IndirectOffsetOnAxis(ap=idx[:, f, t:t + 1], axis=0),
                        ).then_inc(rows_in[g], 16)
            pool.wait_ge(flag_ready, 1)
            outside_found = pool.value_load(flag[0:1, 0:1])
            with pool.If(outside_found > 0):
                with pool.Fori(0, TILES) as t:
                    pool.wait_ge(gidx_ready, t + 1)
                    pool.sem_inc(pool_turn, 1)
                    for f in range(NFEAT):
                        pool.indirect_dma_start(
                            out=grow[:, f, :], out_offset=None, in_=user_rec,
                            in_offset=bass.IndirectOffsetOnAxis(ap=gidx[:, f:f + 1], axis=0),
                        ).then_inc(grow_in, 16)

        @block.scalar
        def _(act):
            act.dma_start(cst[:, :], facts).then_inc(facts_in, 16)
            act.dma_start(w_sb[:, :], weights).then_inc(w_in, 16)
            act.wait_ge(facts_in, 16)
            nc.scalar.copy(Z[:, :, COL_PRICE], pr[:, :]).then_inc(zprice_ready, 1)
            act.wait_ge(scratch_ready, 16)
            spread(act, CHUNK_A + CHUNK_B[2:])

            def small_embeddings(g):
                act.wait_ge(front_read, g + 1)
                nc.scalar.copy(Z[:, tiles(g), COL_SMALL:COL_PRICE],
                               small_ps(g)[:, :, 0:SMALL_EMB]).then_inc(small_read, 1)

            def row_embeddings(g):
                act.wait_ge(rows_in[g], SIZES[g] * 2 * 16)
                nc.scalar.copy(Z[:, tiles(g), 0:2 * E].rearrange("p t (f e) -> p t f e", f=2),
                               rows[:, tiles(g), :, E + 1:REC]).then_inc(zrows_ready, 1)

            def xt_copy(g):
                act.wait_ge(xt_done, g + 1)
                nc.scalar.copy(XT[:, tokens(g)], psX[0:DEEP, 0:SIZES[g] * P]).then_inc(xt_ready, 1)

            def h1_relu(g, c):
                act.wait_ge(h1_done, 2 * g + c + 1)
                nc.scalar.activation(h1[:, c, tokens(g)], psH1[c][:, 0:SIZES[g] * P], ACT.Relu,
                                     bias=par[:, PB1 + c:PB1 + c + 1]).then_inc((h1a_ready, h1b_ready)[c], 1)

            def h2_relu(g):
                act.wait_ge(h2_done, g + 1)
                nc.scalar.activation(h2[:, tokens(g)], psH2[:, 0:SIZES[g] * P], ACT.Relu,
                                     bias=par[:, PB2:PB2 + 1]).then_inc(h2_ready, 1)

            def h3_relu(g):
                act.wait_ge(h3_done, g + 1)
                n = SIZES[g] * H3
                nc.scalar.activation(h3[0:n, g, :], psH3[0:n, 0:P], ACT.Relu,
                                     bias=par[0:n, PB3:PB3 + 1]).then_inc(h3_ready, 1)

            row_embeddings(0)
            small_embeddings(0)
            for g in range(GROUPS + 1):
                if g < GROUPS:
                    xt_copy(g)
                if g + 1 < GROUPS:
                    small_embeddings(g + 1)
                if g >= 1:
                    h2_relu(g - 1)
                if g < GROUPS:
                    h1_relu(g, 0)
                    if g < GROUPS - 1:
                        h1_relu(g, 1)
                if g >= 1:
                    h3_relu(g - 1)
                if g + 1 < GROUPS:
                    row_embeddings(g + 1)

        @block.vector
        def _(dve):
            done = [0]

            def mark(ins):
                ins.then_inc(dve_done, 1)
                done[0] += 1
                return done[0]

            def bt(ap, n):
                return ap.unsqueeze(2).to_broadcast([ap.shape[0], ap.shape[1], n])

            dve.wait_ge(ints_in, 16)
            dve.wait_ge(facts_in, 16)
            m = mark(nc.vector.tensor_tensor(pq[:, :, :], ids[:, :, :], bt(cst[:, C_OFF:C_OFF + NFEAT], TILES), ALU.add))
            dve.wait_ge(dve_done, m)
            nc.vector.tensor_scalar(idx[:, :, :], pq[:, :, :], 0.0, float(2 * NF - 1), ALU.max, ALU.min)\
                .then_inc(idx_ready, 1)

            nslot = NS * TILES
            m = mark(nc.vector.tensor_scalar(sneg[:, :], slot_ids[:, :], 0.0, cst[0:nslot, C_SLOTV:C_SLOTV + 1],
                                             ALU.is_lt, ALU.mult))
            dve.wait_ge(dve_done, m)
            m = mark(nc.vector.tensor_tensor(ssum[:, :], sneg[:, :], slot_ids[:, :], ALU.add))
            dve.wait_ge(dve_done, m)
            m = mark(nc.vector.tensor_scalar(sclip[:, :], ssum[:, :], 0.0, cst[0:nslot, C_SLOTV1:C_SLOTV1 + 1],
                                             ALU.max, ALU.min))
            dve.wait_ge(dve_done, m)
            b0 = (NS - 1) * TILES
            m = mark(nc.vector.tensor_scalar(sclip[b0:nslot, :], sclip[b0:nslot, :], BLOCK_SHIFT, None,
                                             ALU.arith_shift_right))
            dve.wait_ge(dve_done, m)
            nc.vector.tensor_copy(s16[:, :], sclip[:, :]).then_inc(s16_ready, 1)

            dve.wait_ge(tab_in, 16)
            small_tab = tab[:, 0:2 * SMALL_COLS].rearrange("p (a c) -> p a c", a=2)
            brand_tab = tab[:, 2 * SMALL_COLS:TAB_COLS].rearrange("p (a c) -> p a c", a=BLOCK)
            sv = small_tab[:, :, SMALL_EMB:SMALL_EMB + E]
            bv = brand_tab[:, :, BRAND_DIM:BRAND_DIM + E]
            mark(nc.vector.tensor_tensor(tsq[:, 0:2, :], sv, sv, ALU.mult))
            m = mark(nc.vector.tensor_tensor(tsq[:, 2:2 + BLOCK, :], bv, bv, ALU.mult))
            dve.wait_ge(dve_done, m)
            m = mark(nc.vector.reduce_sum(tsum[:, :], tsq[:, :, :], AX))
            dve.wait_ge(dve_done, m)
            sl = small_tab[:, :, SMALL_COLS - 1]
            bl = brand_tab[:, :, BRAND_COLS - 1]
            mark(nc.vector.scalar_tensor_tensor(out=sl, in0=tsum[:, 0:2], scalar=-0.5, in1=sl,
                                                op0=ALU.mult, op1=ALU.add))
            m = mark(nc.vector.scalar_tensor_tensor(out=bl, in0=tsum[:, 2:2 + BLOCK], scalar=-0.5, in1=bl,
                                                    op0=ALU.mult, op1=ALU.add))
            src = tab
            for k in range(3):
                dve.wait_ge(dve_done, m)
                if k == 2:
                    nc.vector.tensor_copy(part[k][:, :], src[:, :]).then_inc(tab_ready, 1)
                    break
                m = mark(nc.vector.tensor_copy(part[k][:, :], src[:, :]))
                dve.wait_ge(dve_done, m)
                m = mark(nc.vector.tensor_tensor(rest[k][:, :], src[:, :], part[k][:, :], ALU.subtract))
                src = rest[k]

            bid = ids[:, BRAND, :]
            m = mark(nc.vector.tensor_scalar(bneg[:, :], bid, 0.0, float(VOCABS[BRAND]), ALU.is_lt, ALU.mult))
            dve.wait_ge(dve_done, m)
            m = mark(nc.vector.tensor_tensor(bsum[:, :], bneg[:, :], bid, ALU.add))
            dve.wait_ge(dve_done, m)
            m = mark(nc.vector.tensor_scalar(bclip[:, :], bsum[:, :], 0.0, float(VOCABS[BRAND] - 1), ALU.max, ALU.min))
            dve.wait_ge(dve_done, m)
            m = mark(nc.vector.tensor_scalar(blow[:, :], bclip[:, :], BLOCK - 1, None, ALU.bitwise_and))
            dve.wait_ge(dve_done, m)
            mask_m = mark(nc.vector.tensor_tensor(
                bmask[:, :, :], bt(blow[:, :], BLOCK),
                cst[:, C_IOTA:C_IOTA + BLOCK].unsqueeze(1).to_broadcast([P, TILES, BLOCK]), ALU.is_equal))

            def weights_of_features():
                mark(nc.vector.tensor_scalar(wrap[:, :, :], pq[:, :, :], float(NF), float(-NF), ALU.is_ge, ALU.mult))
                small_ids = ids[:, 2:NFEAT, :]
                mark(nc.vector.tensor_scalar(below[:, :, :], small_ids, 0.0, None, ALU.is_lt))
                m = mark(nc.vector.tensor_tensor(above[:, :, :], small_ids, bt(cst[:, C_VOC + 2:C_VOC + NFEAT], TILES),
                                                 ALU.is_ge))
                dve.wait_ge(dve_done, m)
                mark(nc.vector.tensor_tensor(pos[:, :, :], pq[:, :, :], wrap[:, :, :], ALU.add))
                m = mark(nc.vector.tensor_tensor(outside[:, :, :], below[:, :, :], above[:, :, :], ALU.max))
                dve.wait_ge(dve_done, m)
                nc.vector.reduce_max(anyout[:, :], outside[:, :, :].rearrange("p f t -> p (f t)"), AX)\
                    .then_inc(anyout_ready, 1)
                mark(nc.vector.tensor_scalar(low_ok[:, :, :], pos[:, :, :], 0.0, None, ALU.is_ge))

                def compare(f):
                    n = NFEAT - 1 - f
                    return mark(nc.vector.tensor_tensor(same[:, f, 0:n, :], pos[:, f + 1:NFEAT, :],
                                                        pos[:, f:f + 1, :].to_broadcast([P, n, TILES]), ALU.is_equal))

                def duplicated(f):
                    n = NFEAT - 1 - f
                    return mark(nc.vector.reduce_max(dup[:, f, :], same[:, f, 0:n, :].rearrange("p g t -> p t g"), AX))

                def weight(f):
                    return mark(nc.vector.scalar_tensor_tensor(out=kept[:, :, f], in0=dup[:, f, :], scalar=0.0,
                                                               in1=valid[:, f, :], op0=ALU.is_equal, op1=ALU.mult))

                compare(0)
                m = compare(1)
                dve.wait_ge(dve_done, m)
                mark(nc.vector.scalar_tensor_tensor(out=valid[:, :, :], in0=pos[:, :, :], scalar=float(NF - 2),
                                                    in1=low_ok[:, :, :], op0=ALU.is_le, op1=ALU.mult))
                duplicated(0)
                m = duplicated(1)
                dve.wait_ge(dve_done, m)
                weight(0)
                weight(1)

            def price_terms():
                vl = lastb[:, 0:E]
                mark(nc.vector.tensor_scalar(prs[:, :], pr[:, :], 0.001, None, ALU.mult))
                mark(nc.vector.tensor_tensor(vlsq[:, :], vl, vl, ALU.mult))
                m = mark(nc.vector.tensor_tensor(bsc[:, :], lastb[:, E + 1:E + 2], lastb[:, E + 2:E + 3], ALU.add))
                dve.wait_ge(dve_done, m)
                mark(nc.vector.tensor_tensor(base[:, :, :], bt(prs[:, :], E + 1),
                                             lastb[:, 0:E + 1].unsqueeze(1).to_broadcast([P, TILES, E + 1]), ALU.mult))
                mark(nc.vector.tensor_tensor(prsq[:, :], prs[:, :], prs[:, :], ALU.mult))
                m = mark(nc.vector.reduce_sum(vlq[:, :], vlsq[:, :], AX))
                dve.wait_ge(dve_done, m)
                m = mark(nc.vector.tensor_scalar(prq[:, :], prsq[:, :], vlq[:, 0:1], -0.5, ALU.mult, ALU.mult))
                dve.wait_ge(dve_done, m)
                return mark(nc.vector.scalar_tensor_tensor(out=base[:, :, E], in0=prq[:, :], scalar=bsc[:, 0:1],
                                                             in1=base[:, :, E], op0=ALU.add, op1=ALU.add))

            def one_hot(b):
                cols = slice(b * OH_BLOCK, (b + 1) * OH_BLOCK)
                for c, n in ((2, P), (0, sum(VOCABS[f] for f in CHUNK_A)), (1, sum(VOCABS[f] for f in CHUNK_B))):
                    if b == 0:
                        dve.wait_ge(idrow_in[c], 16 * (len(CHUNK_A), len(CHUNK_B), 1)[c])
                    nc.vector.tensor_scalar(hot[c][0:n, cols], idrow[c][0:n, cols],
                                            cst[0:n, C_CMP + c:C_CMP + c + 1], None, ALU.is_equal)\
                        .then_inc(hot_ready, 1)

            def flag_copy():
                dve.wait_ge(flag_sum, 1)
                nc.vector.tensor_copy(flag[:, :], psFlag).then_inc(flag_ready, 1)

            def brand_block(g):
                ts = tiles(g)
                dve.wait_ge(front_done, g + 1)
                prod = bprod[:, g % 2, 0:SIZES[g]]
                mark(nc.vector.tensor_tensor(
                    prod.rearrange("p t j c -> p (t j) c"), brand_ps(g).rearrange("p (a c) -> p a c", c=BRAND_COLS),
                    bt(bmask[:, ts, :].rearrange("p t j -> p (t j)"), BRAND_COLS), ALU.mult))
                m = done[0]
                nc.vector.tensor_tensor(front[:, ts, :], small_ps(g)[:, :, SMALL_EMB:SMALL_COLS], base[:, ts, :],
                                        ALU.add).then_inc(front_read, 1)
                dve.wait_ge(dve_done, m)
                for t in range(SIZES[g]):
                    nc.vector.reduce_sum(Z[:, STARTS[g] + t, COL_BRAND:Z_COLS],
                                         prod[:, t].rearrange("p j c -> p c j"), AX).then_inc(brand_ready, 1)

            def h1b(g):
                dve.wait_ge(h1_done, 2 * g + 2)
                nc.vector.tensor_scalar(h1[:, 1, tokens(g)], psH1[1][:, 0:SIZES[g] * P], par[:, PB1 + 1:PB1 + 2],
                                        0.0, ALU.add, ALU.max).then_inc(h1b_ready, 1)

            def machine(g):
                ts = tiles(g)
                dve.wait_ge(rows_in[g], SIZES[g] * 2 * 16)
                w = wrows[:, ts].rearrange("p t f c -> p (t f) c")
                m = mark(nc.vector.tensor_tensor(
                    w, rows[:, ts, :, 0:E + 1].rearrange("p t f c -> p (t f) c"),
                    kept[:, ts, :].rearrange("p t f -> p (t f)").unsqueeze(2).to_broadcast([P, 2 * SIZES[g], E + 1]), ALU.mult))
                dve.wait_ge(dve_done, m)
                mark(nc.vector.tensor_tensor(rsq[:, ts].rearrange("p t f c -> p (t f) c"), w[:, :, 0:E], w[:, :, 0:E],
                                             ALU.mult))
                m = mark(nc.vector.tensor_tensor(S[:, ts, :], wrows[:, ts, 0, :], wrows[:, ts, 1, :], ALU.add))
                dve.wait_ge(dve_done, m)
                mark(nc.vector.reduce_sum(rq[:, ts], rsq[:, ts].rearrange("p t f c -> p t (f c)"), AX))
                m = mark(nc.vector.tensor_tensor(S[:, ts, :], S[:, ts, :], front[:, ts, :], ALU.add))
                dve.wait_ge(dve_done, m)
                m = mark(nc.vector.tensor_tensor(S[:, ts, :], S[:, ts, :], Z[:, ts, DEEP:Z_COLS], ALU.add))
                dve.wait_ge(dve_done, m)
                m = mark(nc.vector.tensor_tensor(ssq[:, ts, :], S[:, ts, 0:E], S[:, ts, 0:E], ALU.mult))
                dve.wait_ge(dve_done, m)
                m = mark(nc.vector.reduce_sum(sq[:, ts], ssq[:, ts, :], AX))
                dve.wait_ge(dve_done, m)
                m = mark(nc.vector.tensor_tensor(sq[:, ts], sq[:, ts], rq[:, ts], ALU.subtract))
                dve.wait_ge(dve_done, m)
                return mark(nc.vector.scalar_tensor_tensor(out=fm[:, ts], in0=sq[:, ts], scalar=0.5,
                                                           in1=S[:, ts, E], op0=ALU.mult, op1=ALU.add))

            weights_of_features()
            one_hot(0)
            m = price_terms()
            dve.wait_ge(dve_done, m)
            brand_block(0)
            brand_block(1)
            one_hot(1)
            for g in range(GROUPS):
                if g == GROUPS - 1:
                    h1b(g)
                if g == 0:
                    flag_copy()
                if g + 2 < GROUPS:
                    brand_block(g + 2)
                if g < 2:
                    one_hot(g + 2)
                m = machine(g)
            dve.wait_ge(dve_done, m)

            outside_found = dve.value_load(flag[0:1, 0:1])
            with dve.If(outside_found > 0):
                step = [0]

                def link(ins):
                    step[0] += 1
                    ins.then_inc(gdve_done, 1)
                    dve.wait_ge(gdve_done, step[0])

                for f in range(NFEAT - 1):
                    n = NFEAT - 1 - f
                    link(nc.vector.tensor_tensor(same[:, f, 0:n, :], pos[:, f + 1:NFEAT, :],
                                                 pos[:, f:f + 1, :].to_broadcast([P, n, TILES]), ALU.is_equal))
                    link(nc.vector.reduce_max(dup[:, f, :], same[:, f, 0:n, :].rearrange("p g t -> p t g"), AX))
                    link(nc.vector.scalar_tensor_tensor(out=gkept[:, :, f], in0=dup[:, f, :], scalar=0.0,
                                                        in1=valid[:, f, :], op0=ALU.is_equal, op1=ALU.mult))
                link(nc.vector.tensor_copy(gkept[:, :, NFEAT - 1], valid[:, NFEAT - 1, :]))
                before, steps = step[0], 10
                with dve.Fori(0, TILES) as t:
                    at = [before]

                    def chain(ins):
                        at[0] += 1
                        ins.then_inc(gdve_done, 1)
                        dve.wait_ge(gdve_done, t * steps + at[0])

                    chain(nc.vector.tensor_copy(gidx[:, :], idx[:, :, bass.ds(t, 1)].rearrange("p f a -> p (f a)")))
                    dve.sem_inc(gidx_ready, 1)
                    dve.wait_ge(grow_in, (t + 1) * (NFEAT * 16))
                    chain(nc.vector.tensor_tensor(
                        gw[:, :, :], grow[:, :, 0:E + 1],
                        gkept[:, bass.ds(t, 1), :].rearrange("p a f -> p (a f)").unsqueeze(2)
                        .to_broadcast([P, NFEAT, E + 1]), ALU.mult))
                    chain(nc.vector.tensor_tensor(gsq[:, :, :], gw[:, :, 0:E], gw[:, :, 0:E], ALU.mult))
                    chain(nc.vector.reduce_sum(gq[:, :], gsq[:, :, :].rearrange("p f c -> p (f c)"), AX))
                    chain(nc.vector.reduce_sum(gsum[:, 0, :], gw[:, :, :].rearrange("p f c -> p c f"), AX))
                    chain(nc.vector.tensor_tensor(gsum[:, :, :], gsum[:, :, :], base[:, bass.ds(t, 1), :], ALU.add))
                    chain(nc.vector.tensor_tensor(gsumsq[:, :], gsum[:, 0, 0:E], gsum[:, 0, 0:E], ALU.mult))
                    chain(nc.vector.reduce_sum(gs[:, :], gsumsq[:, :], AX))
                    chain(nc.vector.tensor_tensor(gs[:, :], gs[:, :], gq[:, :], ALU.subtract))
                    chain(nc.vector.scalar_tensor_tensor(out=fm[:, bass.ds(t, 1)], in0=gs[:, :], scalar=0.5,
                                                         in1=gsum[:, 0, E:E + 1], op0=ALU.mult, op1=ALU.add))
                    assert at[0] - before == steps

            dve.wait_ge(deep_done, GROUPS)
            nc.vector.tensor_tensor(y[:, :], psY[:, 0:TILES], fm[:, :], ALU.add).then_inc(y_ready, 1)

        @block.tensor
        def _(pe):
            def lookups(g):
                if g == 0:
                    pe.wait_ge(tab_ready, 1)
                if g >= 2:
                    pe.wait_ge(small_read, g - 1)
                pe.wait_ge(hot_ready, 3 * (STARTS[g] * P // OH_BLOCK + 1))
                nA, nB = (sum(VOCABS[f] for f in c) for c in (CHUNK_A, CHUNK_B))
                width = BLOCK * BRAND_COLS
                for t in range(SIZES[g]):
                    tok = slice((STARTS[g] + t) * P, (STARTS[g] + t + 1) * P)
                    for k in range(3):
                        nc.tensor.matmul(brand_ps(g)[:, t * width:(t + 1) * width], hot[2][:, tok],
                                         part[k][:, 2 * SMALL_COLS:TAB_COLS], start=(k == 0), stop=(k == 2))
                    for k in range(3):
                        nc.tensor.matmul(small_ps(g)[:, t, :], hot[0][0:nA, tok], part[k][0:nA, 0:SMALL_COLS],
                                         start=(k == 0), stop=False)
                    for k in range(3):
                        last = nc.tensor.matmul(small_ps(g)[:, t, :], hot[1][0:nB, tok],
                                                part[k][0:nB, SMALL_COLS:2 * SMALL_COLS], start=False, stop=(k == 2))
                last.then_inc(front_done, 1)

            def transposes(g):
                pe.wait_ge(brand_ready, STARTS[g] + SIZES[g])
                pe.wait_ge(small_read, g + 1)
                pe.wait_ge(zrows_ready, g + 1)
                if g >= 1:
                    pe.wait_ge(xt_ready, g)
                for t in range(SIZES[g]):
                    last = nc.tensor.transpose(psX[0:DEEP, t * P:(t + 1) * P], Z[:, STARTS[g] + t, 0:DEEP], ident[:, :])
                last.then_inc(xt_done, 1)

            def layer1(g):
                if g >= 1:
                    pe.wait_ge(h1a_ready, g)
                    pe.wait_ge(h1b_ready, g)
                pe.wait_ge(xt_ready, g + 1)
                for c in range(2):
                    nc.tensor.matmul(psH1[c][:, 0:SIZES[g] * P], w1s[:, c * P:(c + 1) * P], XT[:, tokens(g)],
                                     start=True, stop=True).then_inc(h1_done, 1)

            def layer2(g):
                if g >= 1:
                    pe.wait_ge(h2_ready, g)
                n = SIZES[g] * P
                pe.wait_ge(h1a_ready, g + 1)
                nc.tensor.matmul(psH2[:, 0:n], w2s[:, 0, :], h1[:, 0, tokens(g)], start=True, stop=False)
                pe.wait_ge(h1b_ready, g + 1)
                nc.tensor.matmul(psH2[:, 0:n], w2s[:, 1, :], h1[:, 1, tokens(g)], start=False, stop=True)\
                    .then_inc(h2_done, 1)

            def layer3(g):
                if g >= 1:
                    pe.wait_ge(h3_ready, g)
                pe.wait_ge(h2_ready, g + 1)
                for i in range(SIZES[g]):
                    t = STARTS[g] + i
                    last = nc.tensor.matmul(psH3[i * H3:(i + 1) * H3, 0:P], w3s[:, :], h2[:, t * P:(t + 1) * P],
                                            start=True, stop=True)
                last.then_inc(h3_done, 1)

            def layer4(g):
                if g == 0:
                    pe.wait_ge(flag_ready, 1)
                pe.wait_ge(h3_ready, g + 1)
                n = SIZES[g]
                nc.tensor.matmul(psY[:, tiles(g)], h3[0:n * H3, g, :], par[0:n * H3, PWO:PWO + n],
                                 start=True, stop=True).then_inc(deep_done, 1)

            lookups(0)
            lookups(1)
            pe.wait_ge(ident_ready, 1)
            pe.wait_ge(zprice_ready, 1)
            pe.wait_ge(w_in, 16)
            pe.wait_ge(facts_in, 16)
            for g in range(GROUPS + 2):
                if g < GROUPS:
                    transposes(g)
                if 1 <= g <= GROUPS:
                    layer2(g - 1)
                if g >= 2:
                    layer4(g - 2)
                if g < GROUPS:
                    layer1(g)
                if g == 0:
                    pe.wait_ge(ones_ready, 1)
                    pe.wait_ge(anyout_ready, 1)
                    nc.tensor.matmul(psFlag, anyout[:, :], ones[:, :], start=True, stop=True).then_inc(flag_sum, 1)
                if 1 <= g <= GROUPS:
                    layer3(g - 1)
                if g + 2 < GROUPS:
                    lookups(g + 2)


def build(nc, arrays):
    args = {name: nc.dram_tensor(name, a.shape, mybir.dt.from_np(a.dtype), kind="ExternalInput").ap()
            for name, a in arrays.items()}
    scratch = nc.dram_tensor("slot_rows", (len(SLOT_FEATS), BATCH), mybir.dt.float16, kind="Internal").ap()
    out = nc.dram_tensor("out", (BATCH,), mybir.dt.float32, kind="ExternalOutput").ap()
    rec_kernel(nc, scratch=scratch, out=out, **args)


def edge(table, before, after):
    return np.concatenate([np.repeat(table[:1], before, 0), table, np.repeat(table[-1:], after, 0)])


def constants():
    c = np.zeros((P, C_COLS), np.float32)
    for f in range(NFEAT):
        c[:, C_OFF + f] = OFFSET[f] + NF
        c[:, C_VOC + f] = VOCABS[f]
    c[:, C_IOTA:C_IOTA + BLOCK] = np.arange(BLOCK)
    for s, f in enumerate(SLOT_FEATS):
        c[s * TILES:(s + 1) * TILES, C_SLOTV] = VOCABS[f]
        c[s * TILES:(s + 1) * TILES, C_SLOTV1] = VOCABS[f] - 1
    for k, feats in enumerate((CHUNK_A, CHUNK_B)):
        at = 0
        for f in feats:
            c[at:at + VOCABS[f], C_CMP + k] = np.arange(VOCABS[f])
            at += VOCABS[f]
    c[:, C_CMP + 2] = np.arange(P)
    return c


def lay_out(inputs):
    x = {k: np.asarray(v) for k, v in inputs.items()}
    ids = np.stack([x[f"r_{n}_id"] if f"r_{n}_id" in x else x[f"r_{n}"] for n in NAMES])[:, :, 0]
    by_tile = ids.reshape(NFEAT, P, TILES)
    emb = [x[f"L0_rec_emb_{n}"] for n in NAMES]
    fm_v, w_dense = x["L0_rec_fm_v"], x["L0_rec_w_dense"][:, None]

    def records(f):
        v, o = VOCABS[f], OFFSET[f]
        rows = np.concatenate([edge(emb[f], NF + o - v, 0), edge(emb[f], 0, NF - o - v)])
        return np.concatenate([np.concatenate([fm_v, fm_v]), np.concatenate([w_dense, w_dense]), rows], 1)

    tables = np.zeros((P, TAB_COLS), np.float32)
    emb_at = {f: sum(DIMS[g] for g in SMALL[:i]) for i, f in enumerate(SMALL)}
    for k, feats in enumerate((CHUNK_A, CHUNK_B)):
        at, c0 = 0, k * SMALL_COLS
        for f in feats:
            rows = slice(at, at + VOCABS[f])
            here = slice(OFFSET[f], OFFSET[f] + VOCABS[f])
            tables[rows, c0 + emb_at[f]:c0 + emb_at[f] + DIMS[f]] = emb[f]
            tables[rows, c0 + SMALL_EMB:c0 + SMALL_EMB + E] = fm_v[here]
            tables[rows, c0 + SMALL_COLS - 1:c0 + SMALL_COLS] = w_dense[here]
            at += VOCABS[f]
    here = slice(OFFSET[BRAND], OFFSET[BRAND] + VOCABS[BRAND])
    brand = np.concatenate([emb[BRAND], fm_v[here], w_dense[here]], 1)
    tables[0:VOCABS[BRAND] // BLOCK, 2 * SMALL_COLS:] = brand.reshape(VOCABS[BRAND] // BLOCK, BLOCK * BRAND_COLS)

    w1_at = [sum(DIMS[:f]) for f in range(NFEAT + 1)]
    order = [0, 1] + SMALL + [NFEAT] + [BRAND]
    w1 = np.concatenate([x["L0_rec_W1"][w1_at[f]:w1_at[f] + (DIMS + [1])[f]] for f in order])
    weights = np.zeros((P, W_COLS), np.float32)
    weights[0:DEEP, 0:H1] = w1
    weights[:, H1:H1 + 2 * H2] = x["L0_rec_W2"].reshape(2, P, H2).transpose(1, 0, 2).reshape(P, -1)
    weights[:, H1 + 2 * H2:] = x["L0_rec_W3"]
    facts = np.zeros((P, FACTS), np.float32)
    facts[:, 0:C_COLS] = constants()
    facts[:, PB1:PB1 + 2] = x["L0_rec_b1"].reshape(2, P).T
    facts[:, PB2] = x["L0_rec_b2"]
    for i in range(2):
        facts[i * H3:(i + 1) * H3, PB3] = x["L0_rec_b3"]
        facts[i * H3:(i + 1) * H3, PWO + i] = x["L0_rec_Wo"][:, 0]
    facts[:, P_PRICE:P_LAST] = x["r_price"].reshape(P, TILES)
    facts[:, P_LAST:] = np.concatenate([fm_v[-1], w_dense[-1], x["L0_rec_b_dense"].reshape(1), x["L0_rec_bo"]])
    ints = np.zeros((P, INTS), np.int32)
    ints[:, 0:NFEAT * TILES] = by_tile.transpose(1, 0, 2).reshape(P, -1)
    ints[0:len(SLOT_FEATS) * TILES, NFEAT * TILES:] = by_tile[SLOT_FEATS].transpose(0, 2, 1).reshape(-1, P)
    return {
        "ints": ints,
        "facts": facts,
        "user_rec": records(0),
        "item_rec": records(1),
        "tables": tables,
        "weights": weights,
    }


def kernel(**inputs):
    import concourse.bacc as _bacc
    from concourse.bass_utils import run_bass_kernel_spmd as _run

    nc = _bacc.Bacc("TRN2", target_bir_lowering=False, num_devices=1)
    arrays = lay_out(inputs)
    build(nc, arrays)
    r = _run(nc, [arrays], core_ids=[0])
    return r.results[0]["out"]
```

```python
import numpy as np
import concourse.bass as bass
from concourse import mybir
from contextlib import ExitStack

P = 128
BATCH = 2048
TILES = BATCH // P
NAMES = ["user", "item", "age", "gender", "city", "category", "brand", "hour", "device"]
VOCABS = [12500, 6250, 10, 3, 100, 50, 1000, 24, 5]
DIMS = [16, 16, 8, 4, 8, 8, 8, 4, 4]
E = 16
NFEAT = len(NAMES)
NF = sum(VOCABS) + 1
OFFSET = [sum(VOCABS[:i]) for i in range(NFEAT)]
REC = 2 * E + 1
BRAND = NAMES.index("brand")
SMALL = [f for f in range(2, NFEAT) if f != BRAND]
TINY = [NAMES.index("age"), NAMES.index("gender"), NAMES.index("device")]
TINY_ROWS = max(VOCABS[f] for f in TINY)
SLOT_FEATS = TINY + [f for f in SMALL if f not in TINY] + [BRAND]
SMALL_EMB = sum(DIMS[f] for f in SMALL)
SMALL_COLS = SMALL_EMB + E + 1
CHUNK_A = {NAMES.index("city"): 0, NAMES.index("hour"): VOCABS[NAMES.index("city")]}
TINY_AT = VOCABS[NAMES.index("category")]
CHUNK_B = {NAMES.index("category"): 0} | {f: TINY_AT + i * TINY_ROWS for i, f in enumerate(TINY)}
ROWS_A = sum(VOCABS[f] for f in CHUNK_A)
ROWS_B = TINY_AT + len(TINY) * TINY_ROWS
BRAND_DIM = DIMS[BRAND]
BRAND_COLS = BRAND_DIM + E + 1
BLOCK = 8
BLOCK_SHIFT = 3
TAB_COLS = 2 * SMALL_COLS + BLOCK * BRAND_COLS
MACH = E + 1
COL_DEEP = MACH
COL_ITEM = REC
COL_ITEM_MACH = COL_ITEM + E
COL_SMALL = COL_ITEM + REC
COL_PRICE = COL_SMALL + SMALL_EMB
COL_BRAND = COL_PRICE + 1
COL_BRAND_MACH = COL_BRAND + BRAND_DIM
DEEP = COL_BRAND_MACH - COL_DEEP
Z_COLS = COL_BRAND_MACH + MACH
H1, H2, H3 = 256, 128, 64
PAIR = 2
SIZES = [PAIR] * (TILES // PAIR - 1) + [1] * PAIR
STARTS = [sum(SIZES[:g]) for g in range(len(SIZES))]
GROUPS = len(SIZES)
MACHINE_AFTER = {1: (0, 1), 3: (2, 3), 5: (4, 5), 7: (6,), 8: (7, 8)}
HOT_AT = [0, 2, 6, 10, TILES]
C_OFF = 0
C_VOC = C_OFF + NFEAT
C_IOTA = C_VOC + NFEAT
C_SLOTV = C_IOTA + BLOCK
C_SLOTV1 = C_SLOTV + 1
C_CMP = C_SLOTV1 + 1
C_COLS = C_CMP + 3
PB1 = C_COLS
PB2, PB3, PWO = PB1 + 2, PB1 + 3, PB1 + 4
P_PRICE = PWO + 2
P_LAST = P_PRICE + TILES
FACTS = P_LAST + E + 3
INTS = NFEAT * TILES + P
W_COLS = H1 + 2 * H2 + H3


def rec_kernel(nc, ints, facts, user_rec, item_rec, tables, weights, scratch, out):
    fp32, bf16, i32, u8 = mybir.dt.float32, mybir.dt.bfloat16, mybir.dt.int32, mybir.dt.uint8
    ALU = mybir.AluOpType
    ACT = mybir.ActivationFunctionType
    AX = mybir.AxisListType.X
    NS = len(SLOT_FEATS)

    with ExitStack() as ctx:
        def sb(name, shape, dt=fp32):
            return ctx.enter_context(nc.sbuf_tensor(name, shape, dt))

        def ps(name, shape):
            return ctx.enter_context(nc.psum_tensor(name, shape, fp32))

        def sem(name):
            return ctx.enter_context(nc.semaphore(name))

        ints_sb = sb("ints_sb", [P, INTS], i32)
        ids = ints_sb[:, 0:NFEAT * TILES].rearrange("p (f t) -> p f t", f=NFEAT)
        slot_ids = ints_sb[0:NS * TILES, NFEAT * TILES:INTS]
        cst = par = sb("facts_sb", [P, FACTS])
        pr = cst[:, P_PRICE:P_LAST]
        lastb = cst[:, P_LAST:FACTS]
        w_sb = sb("w_sb", [P, W_COLS])
        w1s = w_sb[0:DEEP, 0:H1]
        w2s = w_sb[:, H1:H1 + 2 * H2].rearrange("p (c n) -> p c n", c=2)
        w3s = w_sb[:, H1 + 2 * H2:W_COLS]
        tab = sb("tab", [P, TAB_COLS])
        ident = sb("ident", [P, P])
        ones = sb("ones", [P, 1])
        pq = sb("pq", [P, NFEAT, TILES])
        idx = sb("idx", [P, NFEAT, TILES], i32)
        wrap = sb("wrap", [P, NFEAT, TILES])
        pos = sb("pos", [P, NFEAT, TILES])
        low_ok = sb("low_ok", [P, NFEAT, TILES])
        valid = sb("valid", [P, NFEAT, TILES])
        same = sb("same", [P, NFEAT - 1, NFEAT - 1, TILES])
        dup = sb("dup", [P, NFEAT - 1, TILES])
        kept = sb("kept", [P, TILES, 2])
        bneg = sb("bneg", [P, TILES])
        bsum = sb("bsum", [P, TILES])
        bclip = sb("bclip", [P, TILES], i32)
        blow = sb("blow", [P, TILES], i32)
        bmask = sb("bmask", [P, TILES, BLOCK])
        below = sb("below", [P, NFEAT - 2, TILES])
        above = sb("above", [P, NFEAT - 2, TILES])
        outside = sb("outside", [P, NFEAT - 2, TILES])
        anyout = sb("anyout", [P, 1])
        flag = sb("flag", [1, 1], i32)
        sneg = sb("sneg", [NS * TILES, P])
        ssum = sb("ssum", [NS * TILES, P])
        sclip = sb("sclip", [NS * TILES, P], i32)
        s8 = sb("s8", [NS * TILES, P], u8)
        idrow = [sb(f"idrow{c}", [P, BATCH], u8) for c in range(3)]
        hot = [sb(f"hot{c}", [P, BATCH], bf16) for c in range(3)]
        tsq = sb("tsq", [P, 2 + BLOCK, E])
        tsum = sb("tsum", [P, 2 + BLOCK])
        part = [sb(f"part{k}", [P, TAB_COLS], bf16) for k in range(3)]
        rest = [sb(f"rest{k}", [P, TAB_COLS]) for k in range(2)]
        prs = sb("prs", [P, TILES])
        prsq = sb("prsq", [P, TILES])
        prq = sb("prq", [P, TILES])
        vlsq = sb("vlsq", [P, E])
        vlq = sb("vlq", [P, 1])
        bsc = sb("bsc", [P, 1])
        base = sb("base", [P, TILES, E + 1])
        Z = sb("Z", [P, TILES, Z_COLS])
        XT = sb("XT", [DEEP, BATCH])
        h1 = sb("h1", [P, 2, BATCH])
        h2 = sb("h2", [P, BATCH])
        h3 = sb("h3", [2 * H3, GROUPS, P])
        bprod = sb("bprod", [P, 2, PAIR, BLOCK, BRAND_COLS])
        front = sb("front", [P, TILES, E + 1])
        wrows = sb("wrows", [P, TILES, 2, E + 1])
        rsq = sb("rsq", [P, TILES, 2, E])
        rq = sb("rq", [P, TILES])
        S = sb("S", [P, TILES, E + 1])
        ssq = sb("ssq", [P, TILES, E])
        sq = sb("sq", [P, TILES])
        fm = sb("fm", [P, TILES])
        y = sb("y", [P, TILES])
        gkept = sb("gkept", [P, TILES, NFEAT])
        gidx = sb("gidx", [P, NFEAT], i32)
        grow = sb("grow", [P, NFEAT, REC])
        gw = sb("gw", [P, NFEAT, E + 1])
        gsq = sb("gsq", [P, NFEAT, E])
        gq = sb("gq", [P, 1])
        gsum = sb("gsum", [P, 1, E + 1])
        gsumsq = sb("gsumsq", [P, E])
        gs = sb("gs", [P, 1])

        psF = [ps(f"psF{i}", [P, 512]) for i in range(2)]
        psX = ps("psX", [P, 512])
        psH1 = [ps(f"psH1{c}", [P, 512]) for c in range(2)]
        psH2 = ps("psH2", [P, 512])
        psH3 = ps("psH3", [P, 512])
        psY = ps("psY", [P, 512])
        psFlag = psY[0:1, 511:512]

        def tiles(g):
            return slice(STARTS[g], STARTS[g] + SIZES[g])

        def tokens(g):
            return slice(STARTS[g] * P, (STARTS[g] + SIZES[g]) * P)

        def brand_ps(g):
            return psF[g % 2][:, 0:SIZES[g] * BLOCK * BRAND_COLS]

        def small_ps(g):
            o = PAIR * BLOCK * BRAND_COLS
            return psF[g % 2][:, o:o + SIZES[g] * SMALL_COLS].rearrange("p (t c) -> p t c", t=SIZES[g])

        ints_in = sem("ints_in")
        facts_in = sem("facts_in")
        tab_in = sem("tab_in")
        w_in = sem("w_in")
        dve_done = sem("dve_done")
        idx_ready = sem("idx_ready")
        s8_ready = sem("s8_ready")
        scratch_ready = sem("scratch_ready")
        idrow_in = [sem(f"idrow_in{c}") for c in range(3)]
        hot_ready = sem("hot_ready")
        tab_ready = sem("tab_ready")
        ident0 = sem("ident0")
        ident_ready = sem("ident_ready")
        ones_ready = sem("ones_ready")
        anyout_ready = sem("anyout_ready")
        flag_sum = sem("flag_sum")
        flag_ready = sem("flag_ready")
        zprice_ready = sem("zprice_ready")
        rows_in = [sem(f"rows_in{g}") for g in range(GROUPS)]
        front_done = sem("front_done")
        brand_ready = sem("brand_ready")
        front_read = sem("front_read")
        small_read = sem("small_read")
        xt_done = sem("xt_done")
        xt_ready = sem("xt_ready")
        h1_done = sem("h1_done")
        h1a_ready = sem("h1a_ready")
        h1b_ready = sem("h1b_ready")
        h2_done = sem("h2_done")
        h2_ready = sem("h2_ready")
        h3_done = sem("h3_done")
        h3_ready = sem("h3_ready")
        deep_done = sem("deep_done")
        gidx_ready = sem("gidx_ready")
        grow_in = sem("grow_in")
        pool_turn = sem("pool_turn")
        gdve_done = sem("gdve_done")
        y_ready = sem("y_ready")
        out_done = sem("out_done")

        block = ctx.enter_context(nc.Block())

        def spread(eng, chunk, at, n, f):
            s = SLOT_FEATS.index(f)
            eng.dma_start(idrow[chunk][at:at + n, :], scratch[s:s + 1, :].to_broadcast([n, BATCH]))\
               .then_inc(idrow_in[chunk], 16)

        @block.sync
        def _(sp):
            sp.dma_start(ints_sb[:, :], ints).then_inc(ints_in, 16)
            sp.dma_start(tab[:, :], tables).then_inc(tab_in, 16)
            sp.wait_ge(s8_ready, 1)
            sp.dma_start(scratch.rearrange("f (t p) -> (f t) p", p=P), s8[:, :]).then_inc(scratch_ready, 16)
            sp.wait_ge(scratch_ready, 16)
            spread(sp, 2, 0, P, BRAND)
            category = NAMES.index("category")
            spread(sp, 1, 0, VOCABS[category], category)
            sp.dma_start(idrow[1][TINY_AT:ROWS_B, :],
                         scratch[0:len(TINY), :].unsqueeze(1).to_broadcast([len(TINY), TINY_ROWS, BATCH]))\
              .then_inc(idrow_in[1], 16)
            sp.wait_ge(y_ready, 1)
            sp.dma_start(out.rearrange("(p t) -> p t", t=TILES), y[:, :]).then_inc(out_done, 16)
            sp.wait_ge(out_done, 16)

        @block.gpsimd
        def _(pool):
            nc.gpsimd.memset(ident[:, :], 0.0).then_inc(ident0, 1)
            nc.gpsimd.memset(ones[:, :], 1.0).then_inc(ones_ready, 1)
            pool.wait_ge(ident0, 1)
            nc.gpsimd.affine_select(out=ident[:, :], in_=ident[:, :], compare_op=ALU.not_equal, fill=1.0, base=0,
                                    pattern=[[-1, P]], channel_multiplier=1).then_inc(ident_ready, 1)
            for g in range(GROUPS):
                for t in range(STARTS[g], STARTS[g] + SIZES[g]):
                    for f, table, at in ((0, user_rec, 0), (1, item_rec, COL_ITEM)):
                        if t == 0:
                            pool.wait_ge(idx_ready, f + 1)
                        pool.indirect_dma_start(
                            out=Z[:, t, at:at + REC], out_offset=None, in_=table,
                            in_offset=bass.IndirectOffsetOnAxis(ap=idx[:, f, t:t + 1], axis=0),
                        ).then_inc(rows_in[g], 16)
            pool.wait_ge(flag_ready, 1)
            outside_found = pool.value_load(flag[0:1, 0:1])
            with pool.If(outside_found > 0):
                with pool.Fori(0, TILES) as t:
                    pool.wait_ge(gidx_ready, t + 1)
                    pool.sem_inc(pool_turn, 1)
                    for f in range(NFEAT):
                        pool.indirect_dma_start(
                            out=grow[:, f, :], out_offset=None, in_=user_rec,
                            in_offset=bass.IndirectOffsetOnAxis(ap=gidx[:, f:f + 1], axis=0),
                        ).then_inc(grow_in, 16)

        @block.scalar
        def _(act):
            act.dma_start(cst[:, :], facts).then_inc(facts_in, 16)
            act.dma_start(w_sb[:, :], weights).then_inc(w_in, 16)
            act.wait_ge(facts_in, 16)
            nc.scalar.copy(Z[:, :, COL_PRICE], pr[:, :]).then_inc(zprice_ready, 1)
            act.wait_ge(scratch_ready, 16)
            for f, at in CHUNK_A.items():
                spread(act, 0, at, VOCABS[f], f)

            def small_embeddings(g):
                act.wait_ge(front_read, g + 1)
                nc.scalar.copy(Z[:, tiles(g), COL_SMALL:COL_PRICE],
                               small_ps(g)[:, :, 0:SMALL_EMB]).then_inc(small_read, 1)

            def xt_copy(g):
                act.wait_ge(xt_done, g + 1)
                nc.scalar.copy(XT[:, tokens(g)], psX[0:DEEP, 0:SIZES[g] * P]).then_inc(xt_ready, 1)

            def h1_relu(g, c):
                act.wait_ge(h1_done, 2 * g + c + 1)
                nc.scalar.activation(h1[:, c, tokens(g)], psH1[c][:, 0:SIZES[g] * P], ACT.Relu,
                                     bias=par[:, PB1 + c:PB1 + c + 1]).then_inc((h1a_ready, h1b_ready)[c], 1)

            def h2_relu(g):
                act.wait_ge(h2_done, g + 1)
                nc.scalar.activation(h2[:, tokens(g)], psH2[:, 0:SIZES[g] * P], ACT.Relu,
                                     bias=par[:, PB2:PB2 + 1]).then_inc(h2_ready, 1)

            def h3_relu(g):
                act.wait_ge(h3_done, g + 1)
                n = SIZES[g] * H3
                nc.scalar.activation(h3[0:n, g, :], psH3[0:n, 0:P], ACT.Relu,
                                     bias=par[0:n, PB3:PB3 + 1]).then_inc(h3_ready, 1)

            small_embeddings(0)
            for g in range(GROUPS + 1):
                if g < GROUPS:
                    xt_copy(g)
                if g >= 1:
                    h2_relu(g - 1)
                if g + 1 < GROUPS:
                    small_embeddings(g + 1)
                if g < GROUPS:
                    h1_relu(g, 0)
                    if g < GROUPS - 1:
                        h1_relu(g, 1)
                if g >= 1:
                    h3_relu(g - 1)

        @block.vector
        def _(dve):
            done = [0]

            def mark(ins):
                ins.then_inc(dve_done, 1)
                done[0] += 1
                return done[0]

            def bt(ap, n):
                return ap.unsqueeze(2).to_broadcast([ap.shape[0], ap.shape[1], n])

            dve.wait_ge(ints_in, 16)
            for f in range(2):
                m = mark(nc.vector.tensor_scalar(pq[:, f, :], ids[:, f, :], float(OFFSET[f] + NF), 0.0, ALU.add, ALU.max))
            for f in range(2):
                dve.wait_ge(dve_done, m - 1 + f)
                nc.vector.tensor_scalar(idx[:, f, :], pq[:, f, :], float(2 * NF - 1), None, ALU.min)\
                    .then_inc(idx_ready, 1)

            nslot = NS * TILES
            dve.wait_ge(facts_in, 16)
            m = mark(nc.vector.tensor_scalar(sneg[:, :], slot_ids[:, :], 0.0, cst[0:nslot, C_SLOTV:C_SLOTV + 1],
                                             ALU.is_lt, ALU.mult))
            dve.wait_ge(dve_done, m)
            m = mark(nc.vector.tensor_tensor(ssum[:, :], sneg[:, :], slot_ids[:, :], ALU.add))
            dve.wait_ge(dve_done, m)
            m = mark(nc.vector.tensor_scalar(sclip[:, :], ssum[:, :], 0.0, cst[0:nslot, C_SLOTV1:C_SLOTV1 + 1],
                                             ALU.max, ALU.min))
            dve.wait_ge(dve_done, m)
            b0 = (NS - 1) * TILES
            m = mark(nc.vector.tensor_scalar(sclip[b0:nslot, :], sclip[b0:nslot, :], BLOCK_SHIFT, None,
                                             ALU.arith_shift_right))
            dve.wait_ge(dve_done, m)
            nc.vector.tensor_copy(s8[:, :], sclip[:, :]).then_inc(s8_ready, 1)

            dve.wait_ge(tab_in, 16)
            small_tab = tab[:, 0:2 * SMALL_COLS].rearrange("p (a c) -> p a c", a=2)
            brand_tab = tab[:, 2 * SMALL_COLS:TAB_COLS].rearrange("p (a c) -> p a c", a=BLOCK)
            sv = small_tab[:, :, SMALL_EMB:SMALL_EMB + E]
            bv = brand_tab[:, :, BRAND_DIM:BRAND_DIM + E]
            mark(nc.vector.tensor_tensor(tsq[:, 0:2, :], sv, sv, ALU.mult))
            m = mark(nc.vector.tensor_tensor(tsq[:, 2:2 + BLOCK, :], bv, bv, ALU.mult))
            dve.wait_ge(dve_done, m)
            m = mark(nc.vector.reduce_sum(tsum[:, :], tsq[:, :, :], AX))
            dve.wait_ge(dve_done, m)
            sl = small_tab[:, :, SMALL_COLS - 1]
            bl = brand_tab[:, :, BRAND_COLS - 1]
            mark(nc.vector.scalar_tensor_tensor(out=sl, in0=tsum[:, 0:2], scalar=-0.5, in1=sl,
                                                op0=ALU.mult, op1=ALU.add))
            m = mark(nc.vector.scalar_tensor_tensor(out=bl, in0=tsum[:, 2:2 + BLOCK], scalar=-0.5, in1=bl,
                                                    op0=ALU.mult, op1=ALU.add))
            src = tab
            for k in range(3):
                dve.wait_ge(dve_done, m)
                if k == 2:
                    nc.vector.tensor_copy(part[k][:, :], src[:, :]).then_inc(tab_ready, 1)
                    break
                m = mark(nc.vector.tensor_copy(part[k][:, :], src[:, :]))
                dve.wait_ge(dve_done, m)
                m = mark(nc.vector.tensor_tensor(rest[k][:, :], src[:, :], part[k][:, :], ALU.subtract))
                src = rest[k]

            bid = ids[:, BRAND, :]
            m = mark(nc.vector.tensor_scalar(bneg[:, :], bid, 0.0, float(VOCABS[BRAND]), ALU.is_lt, ALU.mult))
            dve.wait_ge(dve_done, m)
            m = mark(nc.vector.tensor_tensor(bsum[:, :], bneg[:, :], bid, ALU.add))
            dve.wait_ge(dve_done, m)
            m = mark(nc.vector.tensor_scalar(bclip[:, :], bsum[:, :], 0.0, float(VOCABS[BRAND] - 1), ALU.max, ALU.min))
            dve.wait_ge(dve_done, m)
            m = mark(nc.vector.tensor_scalar(blow[:, :], bclip[:, :], BLOCK - 1, None, ALU.bitwise_and))
            dve.wait_ge(dve_done, m)
            mask_m = mark(nc.vector.tensor_tensor(
                bmask[:, :, :], bt(blow[:, :], BLOCK),
                cst[:, C_IOTA:C_IOTA + BLOCK].unsqueeze(1).to_broadcast([P, TILES, BLOCK]), ALU.is_equal))

            def weights_of_features():
                m = mark(nc.vector.tensor_tensor(pq[:, :, :], ids, bt(cst[:, C_OFF:C_OFF + NFEAT], TILES), ALU.add))
                dve.wait_ge(dve_done, m)
                nc.vector.tensor_scalar(idx[:, 2:NFEAT, :], pq[:, 2:NFEAT, :], 0.0, float(2 * NF - 1),
                                        ALU.max, ALU.min).then_inc(idx_ready, 1)
                mark(nc.vector.tensor_scalar(wrap[:, :, :], pq[:, :, :], float(NF), float(-NF), ALU.is_ge, ALU.mult))
                small_ids = ids[:, 2:NFEAT, :]
                mark(nc.vector.tensor_scalar(below[:, :, :], small_ids, 0.0, None, ALU.is_lt))
                m = mark(nc.vector.tensor_tensor(above[:, :, :], small_ids, bt(cst[:, C_VOC + 2:C_VOC + NFEAT], TILES),
                                                 ALU.is_ge))
                dve.wait_ge(dve_done, m)
                mark(nc.vector.tensor_tensor(pos[:, :, :], pq[:, :, :], wrap[:, :, :], ALU.add))
                m = mark(nc.vector.tensor_tensor(outside[:, :, :], below[:, :, :], above[:, :, :], ALU.max))
                dve.wait_ge(dve_done, m)
                nc.vector.reduce_max(anyout[:, :], outside[:, :, :].rearrange("p f t -> p (f t)"), AX)\
                    .then_inc(anyout_ready, 1)
                mark(nc.vector.tensor_scalar(low_ok[:, :, :], pos[:, :, :], 0.0, None, ALU.is_ge))

                def compare(f):
                    n = NFEAT - 1 - f
                    return mark(nc.vector.tensor_tensor(same[:, f, 0:n, :], pos[:, f + 1:NFEAT, :],
                                                        pos[:, f:f + 1, :].to_broadcast([P, n, TILES]), ALU.is_equal))

                return compare(0), compare(1)

            def weights_of_rows(m):
                def duplicated(f):
                    n = NFEAT - 1 - f
                    return mark(nc.vector.reduce_max(dup[:, f, :], same[:, f, 0:n, :].rearrange("p g t -> p t g"), AX))

                def weight(f):
                    return mark(nc.vector.scalar_tensor_tensor(out=kept[:, :, f], in0=dup[:, f, :], scalar=0.0,
                                                               in1=valid[:, f, :], op0=ALU.is_equal, op1=ALU.mult))

                dve.wait_ge(dve_done, m)
                mark(nc.vector.scalar_tensor_tensor(out=valid[:, :, :], in0=pos[:, :, :], scalar=float(NF - 2),
                                                    in1=low_ok[:, :, :], op0=ALU.is_le, op1=ALU.mult))
                duplicated(0)
                m = duplicated(1)
                dve.wait_ge(dve_done, m)
                weight(0)
                return weight(1)

            def price_terms():
                vl = lastb[:, 0:E]
                mark(nc.vector.tensor_scalar(prs[:, :], pr[:, :], 0.001, None, ALU.mult))
                mark(nc.vector.tensor_tensor(vlsq[:, :], vl, vl, ALU.mult))
                m = mark(nc.vector.tensor_tensor(bsc[:, :], lastb[:, E + 1:E + 2], lastb[:, E + 2:E + 3], ALU.add))
                dve.wait_ge(dve_done, m)
                mark(nc.vector.tensor_tensor(base[:, :, :], bt(prs[:, :], E + 1),
                                             lastb[:, 0:E + 1].unsqueeze(1).to_broadcast([P, TILES, E + 1]), ALU.mult))
                mark(nc.vector.tensor_tensor(prsq[:, :], prs[:, :], prs[:, :], ALU.mult))
                m = mark(nc.vector.reduce_sum(vlq[:, :], vlsq[:, :], AX))
                dve.wait_ge(dve_done, m)
                m = mark(nc.vector.tensor_scalar(prq[:, :], prsq[:, :], vlq[:, 0:1], -0.5, ALU.mult, ALU.mult))
                dve.wait_ge(dve_done, m)
                return mark(nc.vector.scalar_tensor_tensor(out=base[:, :, E], in0=prq[:, :], scalar=bsc[:, 0:1],
                                                             in1=base[:, :, E], op0=ALU.add, op1=ALU.add))

            def one_hot(b):
                cols = slice(HOT_AT[b] * P, HOT_AT[b + 1] * P)
                for c, n, loads in ((2, P, 1), (0, ROWS_A, 2), (1, ROWS_B, 2)):
                    if b == 0:
                        dve.wait_ge(idrow_in[c], 16 * loads)
                    nc.vector.tensor_scalar(hot[c][0:n, cols], idrow[c][0:n, cols],
                                            cst[0:n, C_CMP + c:C_CMP + c + 1], None, ALU.is_equal)\
                        .then_inc(hot_ready, 1)

            def flag_copy():
                dve.wait_ge(flag_sum, 1)
                nc.vector.tensor_copy(flag[:, :], psFlag).then_inc(flag_ready, 1)

            def brand_block(g):
                ts = tiles(g)
                dve.wait_ge(front_done, g + 1)
                prod = bprod[:, g % 2, 0:SIZES[g]]
                mark(nc.vector.tensor_tensor(
                    prod.rearrange("p t j c -> p (t j) c"), brand_ps(g).rearrange("p (a c) -> p a c", c=BRAND_COLS),
                    bt(bmask[:, ts, :].rearrange("p t j -> p (t j)"), BRAND_COLS), ALU.mult))
                m = done[0]
                nc.vector.tensor_tensor(front[:, ts, :], small_ps(g)[:, :, SMALL_EMB:SMALL_COLS], base[:, ts, :],
                                        ALU.add).then_inc(front_read, 1)
                dve.wait_ge(dve_done, m)
                for t in range(SIZES[g]):
                    nc.vector.reduce_sum(Z[:, STARTS[g] + t, COL_BRAND:Z_COLS],
                                         prod[:, t].rearrange("p j c -> p c j"), AX).then_inc(brand_ready, 1)

            def h1b(g):
                dve.wait_ge(h1_done, 2 * g + 2)
                nc.vector.tensor_scalar(h1[:, 1, tokens(g)], psH1[1][:, 0:SIZES[g] * P], par[:, PB1 + 1:PB1 + 2],
                                        0.0, ALU.add, ALU.max).then_inc(h1b_ready, 1)

            def machine(groups):
                ts = slice(STARTS[groups[0]], STARTS[groups[-1]] + SIZES[groups[-1]])
                for g in groups:
                    dve.wait_ge(rows_in[g], SIZES[g] * 2 * 16)
                w = wrows[:, ts].rearrange("p t f c -> p (t f) c")
                pair = Z[:, ts, 0:2 * COL_ITEM_MACH].rearrange("p t (f c) -> p t f c", f=2)[:, :, :, 0:MACH]
                m = mark(nc.vector.tensor_tensor(
                    wrows[:, ts], pair, kept[:, ts, :].unsqueeze(3).to_broadcast([P, ts.stop - ts.start, 2, MACH]), ALU.mult))
                dve.wait_ge(dve_done, m)
                mark(nc.vector.tensor_tensor(rsq[:, ts].rearrange("p t f c -> p (t f) c"), w[:, :, 0:E], w[:, :, 0:E],
                                             ALU.mult))
                m = mark(nc.vector.tensor_tensor(S[:, ts, :], wrows[:, ts, 0, :], wrows[:, ts, 1, :], ALU.add))
                dve.wait_ge(dve_done, m)
                mark(nc.vector.reduce_sum(rq[:, ts], rsq[:, ts].rearrange("p t f c -> p t (f c)"), AX))
                m = mark(nc.vector.tensor_tensor(S[:, ts, :], S[:, ts, :], front[:, ts, :], ALU.add))
                dve.wait_ge(dve_done, m)
                m = mark(nc.vector.tensor_tensor(S[:, ts, :], S[:, ts, :], Z[:, ts, COL_BRAND_MACH:Z_COLS], ALU.add))
                dve.wait_ge(dve_done, m)
                m = mark(nc.vector.tensor_tensor(ssq[:, ts, :], S[:, ts, 0:E], S[:, ts, 0:E], ALU.mult))
                dve.wait_ge(dve_done, m)
                m = mark(nc.vector.reduce_sum(sq[:, ts], ssq[:, ts, :], AX))
                dve.wait_ge(dve_done, m)
                m = mark(nc.vector.tensor_tensor(sq[:, ts], sq[:, ts], rq[:, ts], ALU.subtract))
                dve.wait_ge(dve_done, m)
                return mark(nc.vector.scalar_tensor_tensor(out=fm[:, ts], in0=sq[:, ts], scalar=0.5,
                                                           in1=S[:, ts, E], op0=ALU.mult, op1=ALU.add))

            m = price_terms()
            one_hot(0)
            one_hot(1)
            dve.wait_ge(dve_done, m)
            brand_block(0)
            brand_block(1)
            _, compared = weights_of_features()
            m = weights_of_rows(compared)
            dve.wait_ge(dve_done, m)
            for g in range(GROUPS):
                if g == GROUPS - 1:
                    h1b(g)
                if g == 0:
                    flag_copy()
                if g + 2 < GROUPS:
                    brand_block(g + 2)
                if g < 2:
                    one_hot(g + 2)
                if g == GROUPS - 1:
                    dve.wait_ge(flag_ready, 1)
                    outside_found = dve.value_load(flag[0:1, 0:1])
                if g in MACHINE_AFTER:
                    m = machine(MACHINE_AFTER[g])
            dve.wait_ge(dve_done, m)

            with dve.If(outside_found > 0):
                step = [0]

                def link(ins):
                    step[0] += 1
                    ins.then_inc(gdve_done, 1)
                    dve.wait_ge(gdve_done, step[0])

                for f in range(NFEAT - 1):
                    n = NFEAT - 1 - f
                    link(nc.vector.tensor_tensor(same[:, f, 0:n, :], pos[:, f + 1:NFEAT, :],
                                                 pos[:, f:f + 1, :].to_broadcast([P, n, TILES]), ALU.is_equal))
                    link(nc.vector.reduce_max(dup[:, f, :], same[:, f, 0:n, :].rearrange("p g t -> p t g"), AX))
                    link(nc.vector.scalar_tensor_tensor(out=gkept[:, :, f], in0=dup[:, f, :], scalar=0.0,
                                                        in1=valid[:, f, :], op0=ALU.is_equal, op1=ALU.mult))
                link(nc.vector.tensor_copy(gkept[:, :, NFEAT - 1], valid[:, NFEAT - 1, :]))
                before, steps = step[0], 10
                with dve.Fori(0, TILES) as t:
                    at = [before]

                    def chain(ins):
                        at[0] += 1
                        ins.then_inc(gdve_done, 1)
                        dve.wait_ge(gdve_done, t * steps + at[0])

                    chain(nc.vector.tensor_copy(gidx[:, :], idx[:, :, bass.ds(t, 1)].rearrange("p f a -> p (f a)")))
                    dve.sem_inc(gidx_ready, 1)
                    dve.wait_ge(grow_in, (t + 1) * (NFEAT * 16))
                    chain(nc.vector.tensor_tensor(
                        gw[:, :, :], grow[:, :, 0:E + 1],
                        gkept[:, bass.ds(t, 1), :].rearrange("p a f -> p (a f)").unsqueeze(2)
                        .to_broadcast([P, NFEAT, E + 1]), ALU.mult))
                    chain(nc.vector.tensor_tensor(gsq[:, :, :], gw[:, :, 0:E], gw[:, :, 0:E], ALU.mult))
                    chain(nc.vector.reduce_sum(gq[:, :], gsq[:, :, :].rearrange("p f c -> p (f c)"), AX))
                    chain(nc.vector.reduce_sum(gsum[:, 0, :], gw[:, :, :].rearrange("p f c -> p c f"), AX))
                    chain(nc.vector.tensor_tensor(gsum[:, :, :], gsum[:, :, :], base[:, bass.ds(t, 1), :], ALU.add))
                    chain(nc.vector.tensor_tensor(gsumsq[:, :], gsum[:, 0, 0:E], gsum[:, 0, 0:E], ALU.mult))
                    chain(nc.vector.reduce_sum(gs[:, :], gsumsq[:, :], AX))
                    chain(nc.vector.tensor_tensor(gs[:, :], gs[:, :], gq[:, :], ALU.subtract))
                    chain(nc.vector.scalar_tensor_tensor(out=fm[:, bass.ds(t, 1)], in0=gs[:, :], scalar=0.5,
                                                         in1=gsum[:, 0, E:E + 1], op0=ALU.mult, op1=ALU.add))
                    assert at[0] - before == steps

            dve.wait_ge(deep_done, GROUPS)
            nc.vector.tensor_tensor(y[:, :], psY[:, 0:TILES], fm[:, :], ALU.add).then_inc(y_ready, 1)

        @block.tensor
        def _(pe):
            def lookups(g):
                if g == 0:
                    pe.wait_ge(tab_ready, 1)
                if g >= 2:
                    pe.wait_ge(small_read, g - 1)
                before = 3 * sum(a <= STARTS[g] for a in HOT_AT[1:])
                pe.wait_ge(hot_ready, before + 1)
                width = BLOCK * BRAND_COLS
                def token_tile(t):
                    return slice((STARTS[g] + t) * P, (STARTS[g] + t + 1) * P)

                for t in range(SIZES[g]):
                    for k in range(3):
                        nc.tensor.matmul(brand_ps(g)[:, t * width:(t + 1) * width], hot[2][:, token_tile(t)],
                                         part[k][:, 2 * SMALL_COLS:TAB_COLS], start=(k == 0), stop=(k == 2))
                pe.wait_ge(hot_ready, before + 3)
                for t in range(SIZES[g]):
                    for k in range(3):
                        nc.tensor.matmul(small_ps(g)[:, t, :], hot[0][0:ROWS_A, token_tile(t)],
                                         part[k][0:ROWS_A, 0:SMALL_COLS], start=(k == 0), stop=False)
                    for k in range(3):
                        last = nc.tensor.matmul(small_ps(g)[:, t, :], hot[1][0:ROWS_B, token_tile(t)],
                                                part[k][0:ROWS_B, SMALL_COLS:2 * SMALL_COLS],
                                                start=False, stop=(k == 2))
                last.then_inc(front_done, 1)

            def transposes(g):
                pe.wait_ge(brand_ready, STARTS[g] + SIZES[g])
                pe.wait_ge(small_read, g + 1)
                pe.wait_ge(rows_in[g], SIZES[g] * 2 * 16)
                if g >= 1:
                    pe.wait_ge(xt_ready, g)
                for t in range(SIZES[g]):
                    last = nc.tensor.transpose(psX[0:DEEP, t * P:(t + 1) * P],
                                               Z[:, STARTS[g] + t, COL_DEEP:COL_BRAND_MACH], ident[:, :])
                last.then_inc(xt_done, 1)

            def layer1(g):
                if g >= 1:
                    pe.wait_ge(h1a_ready, g)
                    pe.wait_ge(h1b_ready, g)
                pe.wait_ge(xt_ready, g + 1)
                for c in range(2):
                    nc.tensor.matmul(psH1[c][:, 0:SIZES[g] * P], w1s[:, c * P:(c + 1) * P], XT[:, tokens(g)],
                                     start=True, stop=True).then_inc(h1_done, 1)

            def layer2(g):
                if g >= 1:
                    pe.wait_ge(h2_ready, g)
                n = SIZES[g] * P
                pe.wait_ge(h1a_ready, g + 1)
                nc.tensor.matmul(psH2[:, 0:n], w2s[:, 0, :], h1[:, 0, tokens(g)], start=True, stop=False)
                pe.wait_ge(h1b_ready, g + 1)
                nc.tensor.matmul(psH2[:, 0:n], w2s[:, 1, :], h1[:, 1, tokens(g)], start=False, stop=True)\
                    .then_inc(h2_done, 1)

            def layer3(g):
                if g >= 1:
                    pe.wait_ge(h3_ready, g)
                pe.wait_ge(h2_ready, g + 1)
                for i in range(SIZES[g]):
                    t = STARTS[g] + i
                    last = nc.tensor.matmul(psH3[i * H3:(i + 1) * H3, 0:P], w3s[:, :], h2[:, t * P:(t + 1) * P],
                                            start=True, stop=True)
                last.then_inc(h3_done, 1)

            def layer4(g):
                if g == 0:
                    pe.wait_ge(flag_ready, 1)
                pe.wait_ge(h3_ready, g + 1)
                n = SIZES[g]
                nc.tensor.matmul(psY[:, tiles(g)], h3[0:n * H3, g, :], par[0:n * H3, PWO:PWO + n],
                                 start=True, stop=True).then_inc(deep_done, 1)

            lookups(0)
            lookups(1)
            pe.wait_ge(ident_ready, 1)
            pe.wait_ge(zprice_ready, 1)
            pe.wait_ge(w_in, 16)
            pe.wait_ge(facts_in, 16)
            for g in range(GROUPS + 2):
                if g < GROUPS:
                    transposes(g)
                if g == 0:
                    lookups(2)
                if 1 <= g <= GROUPS:
                    layer2(g - 1)
                if g >= 2 and g != GROUPS - 1:
                    layer4(g - 2)
                if g < GROUPS:
                    layer1(g)
                if g == 0:
                    pe.wait_ge(ones_ready, 1)
                    pe.wait_ge(anyout_ready, 1)
                    nc.tensor.matmul(psFlag, anyout[:, :], ones[:, :], start=True, stop=True).then_inc(flag_sum, 1)
                if 1 <= g <= GROUPS:
                    layer3(g - 1)
                if g == GROUPS - 1:
                    layer4(g - 2)
                if 1 <= g < GROUPS - 2:
                    lookups(g + 2)


def build(nc, arrays):
    args = {name: nc.dram_tensor(name, a.shape, mybir.dt.from_np(a.dtype), kind="ExternalInput").ap()
            for name, a in arrays.items()}
    scratch = nc.dram_tensor("slot_rows", (len(SLOT_FEATS), BATCH), mybir.dt.uint8, kind="Internal").ap()
    out = nc.dram_tensor("out", (BATCH,), mybir.dt.float32, kind="ExternalOutput").ap()
    rec_kernel(nc, scratch=scratch, out=out, **args)


def edge(table, before, after):
    return np.concatenate([np.repeat(table[:1], before, 0), table, np.repeat(table[-1:], after, 0)])


def constants():
    c = np.zeros((P, C_COLS), np.float32)
    for f in range(NFEAT):
        c[:, C_OFF + f] = OFFSET[f] + NF
        c[:, C_VOC + f] = VOCABS[f]
    c[:, C_IOTA:C_IOTA + BLOCK] = np.arange(BLOCK)
    for s, f in enumerate(SLOT_FEATS):
        c[s * TILES:(s + 1) * TILES, C_SLOTV] = VOCABS[f]
        c[s * TILES:(s + 1) * TILES, C_SLOTV1] = VOCABS[f] - 1
    c[0:ROWS_B, C_CMP + 1] = -1
    for k, feats in enumerate((CHUNK_A, CHUNK_B)):
        for f, at in feats.items():
            c[at:at + VOCABS[f], C_CMP + k] = np.arange(VOCABS[f])
    c[:, C_CMP + 2] = np.arange(P)
    return c


def lay_out(inputs):
    x = {k: np.asarray(v) for k, v in inputs.items()}
    ids = np.stack([x[f"r_{n}_id"] if f"r_{n}_id" in x else x[f"r_{n}"] for n in NAMES])[:, :, 0]
    by_tile = ids.reshape(NFEAT, P, TILES)
    emb = [x[f"L0_rec_emb_{n}"] for n in NAMES]
    fm_v, w_dense = x["L0_rec_fm_v"], x["L0_rec_w_dense"][:, None]

    def records(f, order):
        v, o = VOCABS[f], OFFSET[f]
        rows = np.concatenate([edge(emb[f], NF + o - v, 0), edge(emb[f], 0, NF - o - v)])
        machine = np.concatenate([fm_v, w_dense], 1)
        parts = {"machine": np.concatenate([machine, machine]), "embedding": rows}
        return np.concatenate([parts[name] for name in order], 1)

    tables = np.zeros((P, TAB_COLS), np.float32)
    emb_at = {f: sum(DIMS[g] for g in SMALL[:i]) for i, f in enumerate(SMALL)}
    for k, feats in enumerate((CHUNK_A, CHUNK_B)):
        c0 = k * SMALL_COLS
        for f, at in feats.items():
            rows = slice(at, at + VOCABS[f])
            here = slice(OFFSET[f], OFFSET[f] + VOCABS[f])
            tables[rows, c0 + emb_at[f]:c0 + emb_at[f] + DIMS[f]] = emb[f]
            tables[rows, c0 + SMALL_EMB:c0 + SMALL_EMB + E] = fm_v[here]
            tables[rows, c0 + SMALL_COLS - 1:c0 + SMALL_COLS] = w_dense[here]
    here = slice(OFFSET[BRAND], OFFSET[BRAND] + VOCABS[BRAND])
    brand = np.concatenate([emb[BRAND], fm_v[here], w_dense[here]], 1)
    tables[0:VOCABS[BRAND] // BLOCK, 2 * SMALL_COLS:] = brand.reshape(VOCABS[BRAND] // BLOCK, BLOCK * BRAND_COLS)

    w1_at = [sum(DIMS[:f]) for f in range(NFEAT + 1)]
    order = [0, 1] + SMALL + [NFEAT] + [BRAND]
    w1 = [x["L0_rec_W1"][w1_at[f]:w1_at[f] + (DIMS + [1])[f]] for f in order]
    w1 = np.concatenate(w1[:2] + [np.zeros((MACH, H1), np.float32)] + w1[2:])
    weights = np.zeros((P, W_COLS), np.float32)
    weights[0:DEEP, 0:H1] = w1
    weights[:, H1:H1 + 2 * H2] = x["L0_rec_W2"].reshape(2, P, H2).transpose(1, 0, 2).reshape(P, -1)
    weights[:, H1 + 2 * H2:] = x["L0_rec_W3"]
    facts = np.zeros((P, FACTS), np.float32)
    facts[:, 0:C_COLS] = constants()
    facts[:, PB1:PB1 + 2] = x["L0_rec_b1"].reshape(2, P).T
    facts[:, PB2] = x["L0_rec_b2"]
    for i in range(2):
        facts[i * H3:(i + 1) * H3, PB3] = x["L0_rec_b3"]
        facts[i * H3:(i + 1) * H3, PWO + i] = x["L0_rec_Wo"][:, 0]
    facts[:, P_PRICE:P_LAST] = x["r_price"].reshape(P, TILES)
    facts[:, P_LAST:] = np.concatenate([fm_v[-1], w_dense[-1], x["L0_rec_b_dense"].reshape(1), x["L0_rec_bo"]])
    ints = np.zeros((P, INTS), np.int32)
    ints[:, 0:NFEAT * TILES] = by_tile.transpose(1, 0, 2).reshape(P, -1)
    ints[0:len(SLOT_FEATS) * TILES, NFEAT * TILES:] = by_tile[SLOT_FEATS].transpose(0, 2, 1).reshape(-1, P)
    return {
        "ints": ints,
        "facts": facts,
        "user_rec": records(0, ("machine", "embedding")),
        "item_rec": records(1, ("embedding", "machine")),
        "tables": tables,
        "weights": weights,
    }


def kernel(**inputs):
    import concourse.bacc as _bacc
    from concourse.bass_utils import run_bass_kernel_spmd as _run

    nc = _bacc.Bacc("TRN2", target_bir_lowering=False, num_devices=1)
    arrays = lay_out(inputs)
    build(nc, arrays)
    r = _run(nc, [arrays], core_ids=[0])
    return r.results[0]["out"]
```
